# Optimizing a Trainium2 kernel written in Bass

```python
import numpy as np
import jax
import jax.numpy as jnp

def _softmax(x, axis=-1):
    return jax.nn.softmax(x, axis=axis)

def _gelu(x):
    return jax.nn.gelu(x, approximate=True)

def _silu(x):
    return jax.nn.silu(x)

def _sigmoid(x):
    return jax.nn.sigmoid(x)

def _layernorm(x, axis=-1, eps=1e-05):
    m = jnp.mean(x, axis=axis, keepdims=True)
    v = jnp.var(x, axis=axis, keepdims=True)
    return (x - m) / jnp.sqrt(v + eps)

def _scatter_add(tgt, idx, src, axis=0):
    return tgt.at[idx].add(src)

def _segment_sum(src, seg, n):
    return jax.ops.segment_sum(src, seg, n)
kernel_name = 'mk_gnn_ffn_d1_gnn_r32_94fe14'

def setup_inputs(seed: int=0):
    np.random.seed(seed)
    _w = jnp.asarray

    def _rec_inputs():
        import jax
        import jax.numpy as jnp
        _gk = jax.random.key(seed)
        x = -6.415e-05 + 1 * jax.random.normal(jax.random.fold_in(_gk, 1), (625, 512), jnp.float32)
        src = jax.random.randint(jax.random.fold_in(_gk, 2), (20000,), 0, 625, jnp.int32)
        dst = jax.random.randint(jax.random.fold_in(_gk, 3), (20000,), 0, 625, jnp.int32)
        _o = jnp.argsort(dst, stable=True)
        src = src[_o]
        dst = dst[_o]
        return (x, src, dst)
    x, src, dst = _rec_inputs()

    def _L0_gnn_setup():
        import jax, jax.numpy as jnp
        import numpy as np
        N = 625
        E_RAND = 4375
        D_IN = 512
        D_OUT = 512
        SLOPE = 0.2
        key = jax.random.key(seed)
        k1, k2, k3, k4 = jax.random.split(key, 4)
        nodes = jax.random.normal(k1, (N, D_IN), dtype=jnp.float32)
        ei = jax.random.randint(k2, (2, E_RAND), 0, N, dtype=jnp.int64)
        loops = jnp.arange(N, dtype=jnp.int64)
        edge_index = jnp.concatenate([ei, jnp.stack([loops, loops])], axis=1)
        W = jax.random.normal(k3, (D_IN, D_OUT), dtype=jnp.float32) * (1.0 / np.sqrt(D_IN))
        b_w = jnp.zeros((D_OUT,), dtype=jnp.float32)
        a = jax.random.normal(k4, (2 * D_OUT,), dtype=jnp.float32) * (1.0 / np.sqrt(2 * D_OUT))
        b_a = jnp.zeros((), dtype=jnp.float32)
        return {'nodes': nodes, 'edge_index': edge_index, 'W': W, 'b_w': b_w, 'a': a, 'b_a': b_a}
    _L0_gnn_all = _L0_gnn_setup()
    _L0_gnn_in = {k: v for k, v in _L0_gnn_all.items() if k in ('W', 'b_w', 'a', 'b_a')}
    del _L0_gnn_all

    def _L0_ffn_setup():
        import jax, jax.numpy as jnp
        import numpy as np
        B, S, H, E, F = (4, 64, 512, 8, 512)
        key = jax.random.key(seed)
        k = jax.random.split(key, 7)
        x = jax.random.normal(k[0], (B, S, H), dtype=jnp.float32)
        Wr = jax.random.normal(k[1], (H, E), dtype=jnp.float32) / np.sqrt(H)
        br = jnp.zeros((E,), dtype=jnp.float32)
        W1 = jax.random.normal(k[2], (E, H, F), dtype=jnp.float32) / np.sqrt(H)
        b1 = jnp.zeros((E, F), dtype=jnp.float32)
        W2 = jax.random.normal(k[3], (E, F, H), dtype=jnp.float32) / np.sqrt(F)
        b2 = jnp.zeros((E, H), dtype=jnp.float32)
        return {'x': x, 'Wr': Wr, 'br': br, 'W1': W1, 'b1': b1, 'W2': W2, 'b2': b2}
    _L0_ffn_all = _L0_ffn_setup()
    _L0_ffn_in = {k: v for k, v in _L0_ffn_all.items() if k in ('Wr', 'br', 'W1', 'b1', 'W2', 'b2')}
    del _L0_ffn_all
    return {'x': x, 'src': src, 'dst': dst, 'L0_gnn_W': _L0_gnn_in['W'], 'L0_gnn_b_w': _L0_gnn_in['b_w'], 'L0_gnn_a': _L0_gnn_in['a'], 'L0_gnn_b_a': _L0_gnn_in['b_a'], 'L0_ffn_Wr': _L0_ffn_in['Wr'], 'L0_ffn_br': _L0_ffn_in['br'], 'L0_ffn_W1': _L0_ffn_in['W1'], 'L0_ffn_b1': _L0_ffn_in['b1'], 'L0_ffn_W2': _L0_ffn_in['W2'], 'L0_ffn_b2': _L0_ffn_in['b2']}

def reference(x, src, dst, L0_gnn_W, L0_gnn_b_w, L0_gnn_a, L0_gnn_b_a, L0_ffn_Wr, L0_ffn_br, L0_ffn_W1, L0_ffn_b1, L0_ffn_W2, L0_ffn_b2):
    import jax
    import jax.numpy as jnp

    def _L0_gnn_ref(nodes, edge_index, W, b_w, a, b_a):
        import jax, jax.numpy as jnp
        import numpy as np
        N = 625
        E_RAND = 4375
        D_IN = 512
        D_OUT = 512
        SLOPE = 0.2
        h = nodes @ W + b_w
        src = edge_index[0]
        dst = edge_index[1]
        s_dst = h @ a[:D_OUT]
        s_src = h @ a[D_OUT:]
        e = jax.nn.leaky_relu(s_dst[dst] + s_src[src] + b_a, negative_slope=SLOPE)
        w = jnp.exp(e)
        denom = jax.ops.segment_sum(w, dst, num_segments=N)
        alpha = w / denom[dst]
        out = jax.ops.segment_sum(alpha[:, None] * h[src], dst, num_segments=N)
        return out

    def _L0_ffn_ref(x, Wr, br, W1, b1, W2, b2):
        import jax, jax.numpy as jnp
        import numpy as np
        B, S, H, E, F = (4, 64, 512, 8, 512)
        b, s, h = x.shape
        xt = x.reshape(-1, h)
        logits = xt @ Wr + br
        probs = jax.nn.softmax(logits, axis=-1)
        G = jnp.max(probs, axis=-1)
        idx = jnp.argmax(probs, axis=-1)
        h1 = jax.nn.relu(jnp.einsum('nh,ehf->nef', xt, W1) + b1)
        eo = jnp.einsum('nef,efh->neh', h1, W2) + b2
        Eout = jnp.take_along_axis(eo, idx[:, None, None], axis=1)[:, 0, :]
        y = G[:, None] * Eout
        return y.reshape(b, s, h)
    edge_index = jnp.stack([src, dst])
    x = x + _L0_gnn_ref(_layernorm(x, axis=-1), edge_index, L0_gnn_W, L0_gnn_b_w, L0_gnn_a, L0_gnn_b_a)
    x = x + _L0_ffn_ref(_layernorm(x, axis=-1)[None], L0_ffn_Wr, L0_ffn_br, L0_ffn_W1, L0_ffn_b1, L0_ffn_W2, L0_ffn_b2)[0]
    return x

_drawn_inputs = setup_inputs


def setup_inputs(seed=0):
    import zlib

    import numpy as np

    out = dict(_drawn_inputs(seed))
    spreads = {'L0_gnn_b_w': (0.0, 0.1),
     'L0_ffn_br': (0.0, 0.1),
     'L0_ffn_b1': (0.0, 0.307),
     'L0_ffn_b2': (0.0, 0.1)}
    factors = {}
    for name, (base, spread) in spreads.items():
        noise = np.random.default_rng([zlib.crc32(name.encode()), seed]).standard_normal(out[name].shape)
        drawn = base * np.exp(spread * noise) if base else spread * noise
        out[name] = jnp.asarray(drawn.astype(out[name].dtype))
    for name, factor in factors.items():
        out[name] = (out[name] * factor).astype(out[name].dtype)
    return out
```

```python
from contextlib import ExitStack

import concourse.bass as bass
from concourse import mybir

F32 = mybir.dt.float32
BF16 = mybir.dt.bfloat16
I32 = mybir.dt.int32
U32 = mybir.dt.uint32
ALU = mybir.AluOpType
ACT = mybir.ActivationFunctionType
AX_X = mybir.AxisListType.X

N = 625
D = 512
E = 20000
NE = 8
NB = 5
BP = N // NB
KB = D // 128
EPS = 1e-5
SLOPE = 0.2
MAX_W = 3e38
MIN_DEN = 1e-38

CH = 128
NCH = -(-E // CH)
TAIL = E - (NCH - 1) * CH
STEP = N * CH // E
WIN = 24
BEFORE = 10
GN = 100
GC = GN // STEP
NG = -(-N // GN)
NP = NG * GN
GW = GN * NB
WC = WIN * NB
RING = 2 * GC
BAT = 5
RB = RING // BAT
OHW = CH + WC

CAP = 128
ROUNDS = -(-N // CAP)
ROW = D + 4
GATE, TOK, MEAN, RSTD = D, D + 1, D + 2, D + 3
FAR = 65536.0
BASE = 4096.0
NO_TOKEN = 1 << 20
WBUF = 4


def gnn_ffn(nc, x, src, dst, w_gnn, b_w, a, b_a, w_r, b_r, w1, b1, w2, b2, out):
    ctx = ExitStack()
    with ctx:
        def sb(name, shape, dt=F32):
            return ctx.enter_context(nc.sbuf_tensor(name, shape, dt))

        def sem(name):
            return ctx.enter_context(nc.semaphore(name))

        rows = sb("rows", [BP, NB, ROW])
        xn = sb("xn", [BP, NB, D])
        xnT = sb("xnT", [128, KB, N])
        hx = sb("hx", [BP, NB, D + 2])
        wexp_xsT = sb("wexp_xsT", [128, NB * NP])
        wexp = wexp_xsT[0:BP, :].rearrange("p (k n) -> p k n", k=NB)
        wt_fill = sb("wt_fill", [128, NB * NP])
        fill = wt_fill[:, 0:ROW]
        wt = wt_fill[0:BP, :].rearrange("p (k n) -> p k n", k=NB)
        e2_wa = sb("e2_wa", [128, 2 * N])
        e2 = e2_wa[0:BP, :].rearrange("p (s n) -> p s n", s=2)
        wa_bc = e2_wa[:, 0:KB * 128].rearrange("p (k n) -> p k n", k=KB)
        wg = sb("wg", [128, KB, D])
        a_bc = sb("a_bc", [128, 2, D])
        bw_bc = sb("bw_bc", [128, D])
        ba_bc = sb("ba_bc", [128, 1])
        wr_sb = sb("wr_sb", [128, KB, NE])
        br_bc = sb("br_bc", [BP, NE])
        b1_row = sb("b1_row", [NE * KB, 128])
        b1T = sb("b1T", [128, NE * KB])
        b2_bc = sb("b2_bc", [128, NE, D])
        w1_sb = sb("w1_sb", [128, WBUF, KB, D])
        w2_sb = sb("w2_sb", [128, WBUF, KB, D])
        ring_xs = sb("ring_xs", [128, RING * OHW // 2])
        ring = ring_xs[:, :].bitcast(BF16).rearrange("p (s w) -> p s w", s=RING)
        xs = ring_xs[:, 0:NE * ROW].rearrange("p (e r) -> p e r", e=NE)
        xs_n, xsT, h1T = (wexp_xsT[:, i * 2 * D:(i + 1) * 2 * D] for i in range(3))
        xs_n = xs_n.rearrange("p (s n) -> p s n", s=2)
        xsT = xsT.rearrange("p (s k n) -> p s k n", s=2, k=KB)
        h1T = h1T.rearrange("p (s k n) -> p s k n", s=2, k=KB)

        edge_i = sb("edge_i", [128, 2, 2, CH], I32)
        edge_f = sb("edge_f", [128, 2, 2, CH])
        key_f = sb("key_f", [128, 2, 2, CH])
        hi_f = sb("hi_f", [128, 2, CH])
        keyT = sb("keyT", [128, 2, NCH])
        keyrel = sb("keyrel", [128, NCH])
        clipped = sb("clipped", [128, NCH])
        shift = sb("shift", [128, NCH])
        iota_b = sb("iota_b", [128, CH], BF16)
        iota_g = sb("iota_g", [128, GW])
        gen_ab = edge_f[:, 0, :, :].rearrange("p s c -> p (s c)").bitcast(BF16)
        gen_a = edge_f[:, 1, 0, :].bitcast(BF16)[:, 0:CH]
        gen_b = gen_ab[:, 0:GW]
        ones_f = sb("ones_f", [128, 128])
        ones_b = sb("ones_b", [128, 128], BF16)
        zeros_b = sb("zeros_b", [128, 512], BF16)
        ident = sb("ident", [128, 128])
        lower = sb("lower", [BP, BP], BF16)
        bad = sb("bad", [128, 1])
        flags = sb("flags", [1, 2], I32)
        stats = sb("stats", [BP, 2, 6])
        mv = sb("mv", [BP, NB, 2])
        rstd1 = sb("rstd1", [BP, NB])
        vare = sb("vare", [BP, NB])
        minus_half = sb("minus_half", [BP, 1])
        wa = sb("wa", [128, KB, 2])
        junk = wexp_xsT[:, 0:D]
        cst = sb("cst", [128, 4])
        s_src = sb("s_src", [BP, 2, NB])
        den = sb("den", [BP, 2, 2])
        first_slot = sb("first_slot", [BP, NB, NE])
        lg = sb("lg", [BP, NB, NE])
        mx = sb("mx", [BP, NB, 1])
        eq = sb("eq", [BP, NB, NE])
        cand = sb("cand", [BP, NB, NE])
        emin = sb("emin", [BP, NB, 1])
        hot = sb("hot", [BP, NB, NE], BF16)
        gate_e = sb("gate_e", [BP, NB, NE])
        gsum = sb("gsum", [BP, NB])
        prod = sb("prod", [BP, NB, NE])
        rank = sb("rank", [BP, NB])
        over = sb("over", [BP, NB])
        slotf = sb("slotf", [BP, NB])
        slot_i = sb("slot_i", [BP, NB], I32)
        novr = sb("novr", [BP, 1])
        xs_dram = nc.dram_tensor("xs_dram", [NE * CAP, ROW], F32, kind="Internal").ap()

        pb = [ctx.enter_context(nc.psum_tensor(f"pb{i}", [128, 512], F32)) for i in range(8)]
        count_bank = [pb[0], pb[1]]
        turn_bank = [pb[2], pb[3]]
        h_bank = [pb[4], pb[5]]
        sdst_bank = pb[6]
        key_bank = pb[7]
        sdst_last = pb[7][:, 384:384 + BP]
        bad_sum = pb[0][0:1, 0:1]
        ssrc_ps = pb[2][0:BP, 0:NB]
        b1_ps = pb[1][:, 0:NE * KB]
        agg_bank = [(pb[2], pb[3]), (pb[4], pb[5])]
        turn2_bank = [pb[6], pb[7]]
        logit_ps = pb[0][0:BP, 0:NB * NE].rearrange("p (b e) -> p b e", b=NB)
        rank_ps = pb[1][0:BP, 0:NB * NE].rearrange("p (b e) -> p b e", b=NB)
        over_sum = pb[0][0:1, 64:65]
        xsT_bank = [pb[0], pb[1]]
        l1_bank = [(pb[2], pb[3]), (pb[6], pb[7])]
        l2_bank = [pb[4], pb[5]]

        x_loaded = [sem(f"x_loaded{b}") for b in range(NB)]
        edges_loaded = sem("edges_loaded")
        edges_padded = sem("edges_padded")
        wg_loaded = sem("wg_loaded")
        a_loaded = sem("a_loaded")
        small_loaded = sem("small_loaded")
        b2_loaded = sem("b2_loaded")
        w_loaded = [sem(f"w_loaded{e}") for e in range(NE)]
        fill_made = sem("fill_made")
        fill_stored = sem("fill_stored")
        pool_chain = sem("pool_chain")
        consts_made = sem("consts_made")
        dve_chain = sem("dve_chain")
        keys_made = sem("keys_made")
        keys_turned = sem("keys_turned")
        keys_copied = sem("keys_copied")
        bad_made = sem("bad_made")
        bad_summed = sem("bad_summed")
        bad_flag = sem("bad_flag")
        xn_ready = sem("xn_ready")
        var_ready = sem("var_ready")
        rstd_ready = sem("rstd_ready")
        xn_turned = sem("xn_turned")
        xnT_ready = sem("xnT_ready")
        wa_ready = sem("wa_ready")
        wa_bc_ready = sem("wa_bc_ready")
        ssrc_done = sem("ssrc_done")
        sdst_done = sem("sdst_done")
        s_src_ready = sem("s_src_ready")
        exp_done = sem("exp_done")
        wexp_ready = sem("wexp_ready")
        h_done = sem("h_done")
        h_copied = sem("h_copied")
        onehots_made = sem("onehots_made")
        onehots_free = sem("onehots_free")
        counts_done = sem("counts_done")
        wt_done = sem("wt_done")
        gen_made = sem("gen_made")
        gen_used = sem("gen_used")
        gen_counted = sem("gen_counted")
        gen_wt = sem("gen_wt")
        agg_done = sem("agg_done")
        agg_used = sem("agg_used")
        xn2_ready = sem("xn2_ready")
        xn2_turned = sem("xn2_turned")
        xn2T_ready = sem("xn2T_ready")
        b1_turned = sem("b1_turned")
        b1T_ready = sem("b1T_ready")
        logits_done = sem("logits_done")
        shifted = sem("shifted")
        gates_exp = sem("gates_exp")
        hot_ready = sem("hot_ready")
        ranks_done = sem("ranks_done")
        over_made = sem("over_made")
        over_summed = sem("over_summed")
        over_flag = sem("over_flag")
        slots_ready = sem("slots_ready")
        rows_scattered = sem("rows_scattered")
        xs_loaded = [sem(f"xs_loaded{e}") for e in range(NE)]
        xs_n_ready = sem("xs_n_ready")
        xs_turned = sem("xs_turned")
        xsT_ready = sem("xsT_ready")
        l1_half = sem("l1_half")
        pool_gate = sem("pool_gate")
        l1_done = sem("l1_done")
        relu_act = sem("relu_act")
        relu_dve = sem("relu_dve")
        l2_done = sem("l2_done")
        b2_sum = sem("b2_sum")
        round_chain = sem("round_chain")
        y_ready = sem("y_ready")
        out_written = sem("out_written")

        block = ctx.enter_context(nc.Block())

        def rows_of(t, b, w=D):
            return t[b * BP:(b + 1) * BP, 0:w]

        @block.sync
        def _(sp):
            for b in range(NB):
                sp.dma_start(rows[:, b, 0:D], rows_of(x, b)).then_inc(x_loaded[b], 16)
            sp.dma_start(wg[:, :, :], w_gnn.rearrange("(k p) n -> p k n", p=128)).then_inc(wg_loaded, 16)

            def load_weights(r, e):
                n = r * NE + e
                if not (isinstance(n, int) and n < WBUF):
                    sp.wait_ge(l2_done, n - WBUF + 1)
                sp.dma_start(w1_sb[:, e % WBUF, :, :],
                             w1[e].rearrange("(k p) f -> p k f", p=128)).then_inc(w_loaded[e], 16)
                sp.dma_start(w2_sb[:, e % WBUF, :, :],
                             w2[e].rearrange("(k p) f -> p k f", p=128)).then_inc(w_loaded[e], 16)

            def load_slots(r):
                sp.wait_ge(rows_scattered, (r + 1) * (16 * NB))
                for e in range(NE):
                    sp.dma_start(xs[:, e, :], xs_dram[e * CAP:(e + 1) * CAP, :]).then_inc(xs_loaded[e], 16)

            for e in range(WBUF):
                load_weights(0, e)
            load_slots(0)
            for e in range(WBUF, NE):
                load_weights(0, e)

            sp.wait_ge(over_flag, 1)
            more = sp.value_load(flags[0:1, 1:2])
            with sp.If(more != 0):
                with sp.Fori(1, ROUNDS) as r:
                    for e in range(WBUF):
                        load_weights(r, e)
                    sp.wait_ge(out_written, r * (16 * NE))
                    load_slots(r)
                    for e in range(WBUF, NE):
                        load_weights(r, e)

        @block.gpsimd
        def _(pool):
            chain = [0]

            def link(ins):
                chain[0] += 1
                ins.then_inc(pool_chain, 1)
                pool.wait_ge(pool_chain, chain[0])

            nc.gpsimd.memset(edge_i[:, 0, 1, :], -1).then_inc(edges_padded, 1)
            nc.gpsimd.memset(edge_i[:, 1, 1, :], N - 1).then_inc(edges_padded, 1)
            nc.gpsimd.memset(ones_f[:, :], 1.0)
            link(nc.gpsimd.memset(ident[:, :], 0.0))
            nc.gpsimd.affine_select(out=ident[:, :], in_=ident[:, :], compare_op=ALU.not_equal, fill=1.0,
                                    base=0, pattern=[[-1, 128]], channel_multiplier=1).then_inc(consts_made, 1)
            nc.gpsimd.iota(iota_b[:, :], pattern=[[1, CH]], base=0, channel_multiplier=0,
                           allow_small_or_imprecise_dtypes=True)
            nc.gpsimd.iota(shift[:, :], pattern=[[STEP * NB, NCH]], base=-BEFORE * NB, channel_multiplier=0,
                           allow_small_or_imprecise_dtypes=True).then_inc(consts_made, 1)
            def inv_std(b, which, to):
                pool.wait_ge(var_ready, which * NB + b + 1)
                link(nc.gpsimd.tensor_scalar(vare[:, b:b + 1], mv[:, b, 1:2], EPS, None, ALU.add))
                nc.gpsimd.tensor_tensor(to, vare[:, b:b + 1], minus_half[:, :], ALU.pow).then_inc(rstd_ready, 1)

            link(nc.gpsimd.memset(minus_half[:, :], -0.5))

            for b in range(NB):
                inv_std(b, 0, rstd1[:, b:b + 1])
            pool.wait_ge(wa_ready, 1)
            for k in range(KB):
                last = nc.gpsimd.tensor_scalar(wa_bc[:, k, :], ones_f[:, :], wa[:, k, 0:1], None, ALU.mult)
            last.then_inc(wa_bc_ready, 1)
            nc.gpsimd.memset(zeros_b[:, :], 0.0)
            nc.gpsimd.memset(ones_b[:, :], 1.0).then_inc(consts_made, 1)
            nc.gpsimd.memset(wexp[:, :, N:NP], 0.0)
            nc.gpsimd.memset(hx[:, :, D:D + 1], 1.0).then_inc(consts_made, 1)
            nc.gpsimd.memset(fill[:, :], 0.0).then_inc(pool_chain, 1)
            chain[0] += 1
            pool.wait_ge(pool_chain, chain[0])
            nc.gpsimd.memset(fill[:, TOK:TOK + 1].bitcast(I32), NO_TOKEN).then_inc(fill_made, 1)
            nc.gpsimd.iota(rows[:, :, TOK:TOK + 1].bitcast(I32), pattern=[[BP, NB], [0, 1]], base=0, channel_multiplier=1)
            nc.gpsimd.iota(first_slot[:, :, :], pattern=[[0, NB], [CAP, NE]], base=0, channel_multiplier=0,
                           allow_small_or_imprecise_dtypes=True)
            nc.gpsimd.iota(iota_g[:, :], pattern=[[1, GW]], base=0, channel_multiplier=0,
                           allow_small_or_imprecise_dtypes=True)
            link(nc.gpsimd.memset(lower[:, :], 1.0))
            nc.gpsimd.affine_select(out=lower[:, :], in_=lower[:, :], compare_op=ALU.is_gt, fill=0.0,
                                    base=0, pattern=[[1, BP]], channel_multiplier=-1).then_inc(consts_made, 1)

            for b in range(NB):
                inv_std(b, 1, rows[:, b, RSTD:RSTD + 1])
            slot_bound = pool.to_reg(NE * CAP - 1)
            token_bound = pool.to_reg(N - 1)

            def scatter_rows(r):
                pool.wait_ge(slots_ready, r + 1)
                pool.sem_inc(pool_gate, 1)
                for b in range(NB):
                    pool.indirect_dma_start(
                        out=xs_dram, out_offset=bass.IndirectOffsetOnAxis(ap=slot_i[:, b:b + 1].bitcast(U32), axis=0),
                        in_=rows[:, b, :], in_offset=None, bounds_check=slot_bound,
                        oob_is_err=False).then_inc(rows_scattered, 16)

            def scatter_out(r):
                for e in range(NE):
                    pool.wait_ge(y_ready, r * NE + e + 1)
                    pool.sem_inc(pool_gate, 1)
                    pool.indirect_dma_start(
                        out=out, out_offset=bass.IndirectOffsetOnAxis(ap=xs[:, e, TOK:TOK + 1].bitcast(U32), axis=0),
                        in_=xs[:, e, 0:D], in_offset=None, bounds_check=token_bound,
                        oob_is_err=False).then_inc(out_written, 16)

            pool.wait_ge(fill_stored, 16)
            scatter_rows(0)
            scatter_out(0)
            pool.wait_ge(out_written, 16 * NE)
            pool.wait_ge(over_flag, 1)
            more = pool.value_load(flags[0:1, 1:2])
            with pool.If(more != 0):
                with pool.Fori(1, ROUNDS) as r:
                    scatter_rows(r)
                    scatter_out(r)
                    pool.wait_ge(out_written, r * (16 * NE) + 16 * NE)
                nc.gpsimd.engine_nop()

        @block.scalar
        def _(act):
            act.wait_ge(edges_padded, 2)
            ef = NCH - 1 - 128
            for s, t in enumerate((src, dst)):
                act.dma_start(edge_i[:, s, 0, :], t[0:128 * CH].rearrange("(p c) -> p c", c=CH)).then_inc(edges_loaded, 16)
                act.dma_start(edge_i[0:ef, s, 1, :],
                              t[128 * CH:(NCH - 1) * CH].rearrange("(p c) -> p c", c=CH)).then_inc(edges_loaded, 16)
                act.dma_start(edge_i[ef:ef + 1, s, 1, 0:TAIL], t[(NCH - 1) * CH:E].unsqueeze(0)).then_inc(edges_loaded, 16)
            act.dma_start(a_bc[:, :, :], a.rearrange("(t n) -> t n", t=2).partition_broadcast(128)).then_inc(a_loaded, 16)
            act.dma_start(bw_bc[:, :], b_w.partition_broadcast(128)).then_inc(a_loaded, 16)
            act.dma_start(ba_bc[:, :], b_a.partition_broadcast(128)).then_inc(a_loaded, 16)
            act.dma_start(wr_sb[:, :, :], w_r.rearrange("(k p) n -> p k n", p=128)).then_inc(small_loaded, 16)
            act.dma_start(br_bc[:, :], b_r.partition_broadcast(BP)).then_inc(small_loaded, 16)
            act.dma_start(b1_row[:, :], b1.rearrange("e (k p) -> (e k) p", p=128)).then_inc(small_loaded, 16)

            act.wait_ge(keys_turned, 1)
            nc.scalar.copy(keyT[:, :, :], key_bank[:, 0:2 * NCH].rearrange("p (s c) -> p s c", s=2)).then_inc(keys_copied, 1)
            for b in range(NB):
                act.wait_ge(xn_turned, b + 1)
                nc.scalar.copy(xnT[:, :, b * BP:(b + 1) * BP],
                               turn_bank[b % 2][:, 0:KB * BP].rearrange("p (k n) -> p k n", k=KB)).then_inc(xnT_ready, 1)
            act.wait_ge(b1_turned, 1)
            nc.scalar.copy(b1T[:, :], b1_ps).then_inc(b1T_ready, 1)
            act.wait_ge(fill_made, 1)
            act.dma_start(xs_dram.rearrange("(e p) r -> p e r", p=CAP),
                          fill[:, :].unsqueeze(1).to_broadcast([128, NE, ROW])).then_inc(fill_stored, 16)
            act.dma_start(b2_bc[:, :, :], b2.partition_broadcast(128)).then_inc(b2_loaded, 16)
            act.wait_ge(s_src_ready, 1)
            act.wait_ge(sdst_done, 1)
            n0 = 4 * BP
            for k in range(NB):
                if k >= 2:
                    act.wait_ge(wexp_ready, k - 1)
                nc.scalar.activation(wexp[:, k, 0:n0], sdst_bank[0:BP, 0:n0], ACT.Exp, bias=s_src[:, 0, k:k + 1])
                nc.scalar.activation(wexp[:, k, n0:N], sdst_last[0:BP, :], ACT.Exp,
                                     bias=s_src[:, 0, k:k + 1]).then_inc(exp_done, 1)
                nc.scalar.activation(e2[:, k % 2, 0:n0], sdst_bank[0:BP, 0:n0], ACT.Exp,
                                     bias=s_src[:, 1, k:k + 1], scale=SLOPE)
                nc.scalar.activation(e2[:, k % 2, n0:N], sdst_last[0:BP, :], ACT.Exp,
                                     bias=s_src[:, 1, k:k + 1], scale=SLOPE).then_inc(exp_done, 1)
                act.wait_ge(h_done, k + 1)
                nc.scalar.copy(hx[:, k, 0:D], h_bank[k % 2][0:BP, :]).then_inc(h_copied, 1)
            for b in range(NB):
                act.wait_ge(xn2_turned, b + 1)
                nc.scalar.copy(xnT[:, :, b * BP:(b + 1) * BP],
                               turn2_bank[b % 2][:, 0:KB * BP].rearrange("p (k n) -> p k n", k=KB)).then_inc(xn2T_ready, 1)
            act.wait_ge(shifted, 1)
            nc.scalar.activation(gate_e[:, :, :], eq[:, :, :], ACT.Exp).then_inc(gates_exp, 1)

            def round_act(r):
                for e in range(NE):
                    def n(back=0):
                        return r * NE + e + 1 - back
                    act.wait_ge(xs_turned, n())
                    if not (isinstance(r, int) and e < 2):
                        act.wait_ge(l1_done, n(2))
                    nc.scalar.copy(xsT[:, e % 2, :, :],
                                   xsT_bank[e % 2][:, :].rearrange("p (k n) -> p k n", k=KB)).then_inc(xsT_ready, 1)
                    if e >= 1:
                        relu(r, e - 1)
                relu(r, NE - 1)

            def relu(r, e):
                act.wait_ge(l1_half, r * NE + e + 1)
                if not (isinstance(r, int) and e < 2):
                    act.wait_ge(l2_done, r * NE + e - 1)
                for f in range(2):
                    last = nc.scalar.activation(h1T[:, e % 2, f, :], l1_bank[e % 2][0][:, f * CAP:(f + 1) * CAP], ACT.Relu,
                                                bias=b1T[:, e * KB + f:e * KB + f + 1])
                last.then_inc(relu_act, 1)

            round_act(0)
            act.wait_ge(over_flag, 1)
            more = act.value_load(flags[0:1, 1:2])
            with act.If(more != 0):
                with act.Fori(1, ROUNDS) as r:
                    round_act(r)

        @block.vector
        def _(dve):
            chain = [0]

            def link(ins):
                chain[0] += 1
                ins.then_inc(dve_chain, 1)
                dve.wait_ge(dve_chain, chain[0])

            dve.sem_inc(onehots_free, RB)
            dve.sem_inc(wt_done, 1)
            dve.wait_ge(edges_loaded, 6 * 16)
            link(nc.vector.tensor_copy(edge_f[:, :, :, :], edge_i[:, :, :, :]))
            srcf, dstf = edge_f[:, 0, :, :], edge_f[:, 1, :, :]
            link(nc.vector.tensor_scalar(hi_f[:, :, :], srcf, float(BP), None, ALU.is_ge))
            for k in range(2, NB):
                link(nc.vector.scalar_tensor_tensor(hi_f[:, :, :], srcf, float(BP * k), hi_f[:, :, :], ALU.is_ge, ALU.add))
            nc.vector.scalar_tensor_tensor(key_f[:, 0, :, :], hi_f[:, :, :], -float(BP), srcf, ALU.mult, ALU.add)
            nc.vector.scalar_tensor_tensor(key_f[:, 1, :, :], dstf, float(NB), hi_f[:, :, :], ALU.mult,
                                           ALU.add).then_inc(keys_made, 1)

            def row_stats(b):
                link(nc.vector.bn_stats(stats[:, b % 2, :], rows[:, b, 0:D]))
                return nc.vector.bn_aggr(mv[:, b, :], stats[:, b % 2, :])

            def normalise_block(b, which, rstd):
                dve.wait_ge(rstd_ready, which * NB + b + 1)
                nc.vector.tensor_scalar(xn[:, b, :], rows[:, b, 0:D], mv[:, b, 0:1], rstd, ALU.subtract,
                                        ALU.mult).then_inc(xn2_ready if which else xn_ready, 1)

            def project_a(k):
                for t in range(2):
                    link(nc.vector.tensor_tensor_reduce(out=junk[:, :], in0=wg[:, k, :], in1=a_bc[:, t, :], scale=1.0,
                                                        scalar=0.0, op0=ALU.mult, op1=ALU.add, accum_out=wa[:, k, t:t + 1]))

            for b in range(NB):
                dve.wait_ge(x_loaded[b], 16)
                row_stats(b).then_inc(var_ready, 1)
                if b >= 1:
                    normalise_block(b - 1, 0, rstd1[:, b - 1:b])
                if b == 1:
                    dve.wait_ge(keys_copied, 1)
                    dve.wait_ge(consts_made, 2)
                    link(nc.vector.tensor_tensor(keyrel[:, :], keyT[:, 1, :], shift[:, :], ALU.subtract))
                    link(nc.vector.tensor_scalar(clipped[:, :], keyrel[:, :], 0.0, float(WC - 1), ALU.max, ALU.min))
                    link(nc.vector.tensor_tensor(clipped[:, :], clipped[:, :], keyrel[:, :], ALU.not_equal))
                    nc.vector.tensor_reduce(bad[:, :], clipped[:, :], AX_X, ALU.add).then_inc(bad_made, 1)
            normalise_block(NB - 1, 0, rstd1[:, NB - 1:NB])
            dve.wait_ge(wg_loaded, 16)
            dve.wait_ge(a_loaded, 48)
            for k in range(KB):
                project_a(k)
            for t in range(2):
                link(nc.vector.tensor_tensor_reduce(out=junk[:, :], in0=bw_bc[:, :], in1=a_bc[:, t, :], scale=1.0,
                                                    scalar=0.0, op0=ALU.mult, op1=ALU.add, accum_out=cst[:, t:t + 1]))
            dve.sem_inc(wa_ready, 1)
            link(nc.vector.tensor_tensor(cst[:, 2:3], cst[:, 0:1], cst[:, 1:2], ALU.add))
            link(nc.vector.tensor_tensor(cst[:, 3:4], cst[:, 2:3], ba_bc[:, :], ALU.add))
            dve.wait_ge(bad_summed, 1)
            nc.vector.tensor_copy(flags[0:1, 0:1], bad_sum).then_inc(bad_flag, 1)

            def onehots(i, j):
                c = i * RING + j
                s = j % RING
                if j % BAT == 0:
                    dve.wait_ge(onehots_free, i * RB + j // BAT + 1)
                nc.vector.tensor_scalar(ring[:, s, 0:CH], iota_b[:, :], keyT[:, 0, bass.ds(c, 1)], None, ALU.is_equal)
                ins = nc.vector.tensor_scalar(ring[:, s, CH:OHW], iota_b[:, 0:WC], keyrel[:, bass.ds(c, 1)], None,
                                              ALU.is_equal)
                if j % BAT == BAT - 1 or (isinstance(c, int) and c == NCH - 1):
                    ins.then_inc(onehots_made, 1)

            def weigh(g, ready, ps, done):
                at = bass.ds(g * GN, GN)
                dve.wait_ge(*ready)
                nc.vector.scalar_tensor_tensor(wt[:, :, at], wexp[:, :, at], MAX_W,
                                               ps[0:BP, 0:GW].rearrange("p (n k) -> p k n", k=NB),
                                               ALU.min, ALU.mult).then_inc(done, 1)

            def weigh_band(g, parity):
                weigh(g, (counts_done, g + 2), count_bank[parity], wt_done)

            lead = 3 * BAT
            for j in range(lead):
                onehots(0, j)
            dve.wait_ge(ssrc_done, 1)
            link(nc.vector.tensor_scalar(s_src[:, 0, :], ssrc_ps, cst[0:BP, 3:4], None, ALU.add))
            nc.vector.tensor_scalar(s_src[:, 1, :], s_src[:, 0, :], SLOPE, None, ALU.mult).then_inc(s_src_ready, 1)
            for j in range(lead, GC + lead):
                onehots(0, j)
                if j % BAT == BAT - 1:
                    k = (j - lead) // BAT
                    dve.wait_ge(exp_done, 2 * (k + 1))
                    nc.vector.tensor_tensor(wexp[:, k, 0:N], wexp[:, k, 0:N], e2[:, k % 2, :],
                                            ALU.max).then_inc(wexp_ready, 1)
            dve.wait_ge(wexp_ready, NB)
            dve.wait_ge(consts_made, 4)
            dve.wait_ge(fill_stored, 16)
            weigh_band(0, 0)
            with dve.Fori(0, 2) as i:
                for j in range(GC + lead, 3 * GC + lead):
                    onehots(i, j)
                    if j == 2 * GC + lead - 1:
                        weigh_band(2 * i + 1, 1)
                weigh_band(2 * i + 2, 0)
            for j in range(GC + lead, NCH - 2 * RING):
                onehots(2, j)
            weigh_band(5, 1)
            weigh_band(6, 0)

            dve.wait_ge(bad_flag, 1)
            outside = dve.value_load(flags[0:1, 0:1])
            with dve.If(outside != 0):
                dve.wait_ge(wt_done, NG + 1)
                dve.wait_ge(consts_made, 5)
                dve.sem_inc(gen_used, 1)
                dve.sem_inc(gen_wt, 1)
                with dve.Fori(0, NG) as g:
                    with dve.Fori(0, NCH) as c:
                        dve.wait_ge(gen_used, g * NCH + c + 1)
                        nc.vector.tensor_scalar(gen_a[:, :], iota_b[:, :], keyT[:, 0, bass.ds(c, 1)], None, ALU.is_equal)
                        nc.vector.tensor_scalar(gen_b[:, :], iota_g[:, :], keyT[:, 1, bass.ds(c, 1)], None,
                                                ALU.is_equal).then_inc(gen_made, 1)
                    weigh(g, (gen_counted, g + 1), count_bank[0], gen_wt)
                    nc.vector.tensor_scalar(keyT[:, 1, :], keyT[:, 1, :], -float(GW), None, ALU.add).then_inc(gen_wt, 1)
                    dve.wait_ge(gen_wt, g * 2 + 3)

            dve.wait_ge(xn_turned, NB)
            for b in range(NB):
                pa, pc = agg_bank[b % 2]
                dve.wait_ge(agg_done, b + 1)
                link(nc.vector.tensor_scalar(den[:, b % 2, 0:1], pa[0:BP, 256:257], MIN_DEN, None, ALU.max))
                link(nc.vector.reciprocal(den[:, b % 2, 1:2], den[:, b % 2, 0:1]))
                nc.vector.scalar_tensor_tensor(rows[:, b, 0:256], pc[0:BP, 0:256], den[:, b % 2, 1:2], rows[:, b, 0:256],
                                               ALU.mult, ALU.add)
                link(nc.vector.scalar_tensor_tensor(rows[:, b, 256:512], pa[0:BP, 0:256], den[:, b % 2, 1:2],
                                                    rows[:, b, 256:512], ALU.mult, ALU.add))
                dve.sem_inc(agg_used, 1)
                row_stats(b).then_inc(var_ready, 1)
                if b >= 1:
                    normalise_block(b - 1, 1, rows[:, b - 1, RSTD:RSTD + 1])
            normalise_block(NB - 1, 1, rows[:, NB - 1, RSTD:RSTD + 1])
            nc.vector.tensor_copy(rows[:, :, MEAN:MEAN + 1], mv[:, :, 0:1])

            def over_e(t):
                return t[:, :, 0:1].to_broadcast([BP, NB, NE])
            dve.wait_ge(small_loaded, 48)
            dve.wait_ge(consts_made, 5)
            dve.wait_ge(logits_done, 1)
            link(nc.vector.tensor_tensor(lg[:, :, :], logit_ps, br_bc[:, :].unsqueeze(1).to_broadcast([BP, NB, NE]), ALU.add))
            link(nc.vector.tensor_reduce(mx[:, :, :], lg[:, :, :], AX_X, ALU.max))
            link(nc.vector.tensor_tensor(eq[:, :, :], lg[:, :, :], over_e(mx), ALU.is_equal))
            link(nc.vector.scalar_tensor_tensor(cand[:, :, :], eq[:, :, :], -BASE, first_slot[:, :, :], ALU.mult, ALU.add))
            link(nc.vector.tensor_reduce(emin[:, :, :], cand[:, :, :], AX_X, ALU.min))
            nc.vector.tensor_tensor(hot[:, :, :], cand[:, :, :], over_e(emin), ALU.is_equal).then_inc(hot_ready, 1)
            nc.vector.tensor_tensor(eq[:, :, :], lg[:, :, :], over_e(mx), ALU.subtract).then_inc(shifted, 1)
            dve.wait_ge(gates_exp, 1)
            link(nc.vector.tensor_reduce(gsum[:, :], gate_e[:, :, :], AX_X, ALU.add))
            link(nc.vector.reciprocal(rows[:, :, GATE:GATE + 1], gsum[:, :].unsqueeze(2)))
            dve.wait_ge(ranks_done, 1)
            link(nc.vector.tensor_tensor(prod[:, :, :], rank_ps, hot[:, :, :], ALU.mult))
            link(nc.vector.tensor_reduce(rank[:, :], prod[:, :, :], AX_X, ALU.add))

            emin2 = emin[:, :, :].rearrange("p b o -> p (b o)")
            link(nc.vector.tensor_scalar(over[:, :], rank[:, :], float(CAP), FAR, ALU.is_ge, ALU.mult))
            link(nc.vector.scalar_tensor_tensor(slotf[:, :], rank[:, :], BASE, over[:, :], ALU.add, ALU.add))
            nc.vector.tensor_tensor(slot_i[:, :], slotf[:, :], emin2, ALU.add).then_inc(slots_ready, 1)
            nc.vector.tensor_reduce(novr[:, :], over[:, :], AX_X, ALU.add).then_inc(over_made, 1)
            dve.wait_ge(over_summed, 1)
            nc.vector.tensor_copy(flags[0:1, 1:2], over_sum).then_inc(over_flag, 1)

            def round_dve(r, step):
                static = isinstance(r, int)

                def n(e):
                    return r * NE + e + 1

                def normalise(e):
                    dve.wait_ge(xs_loaded[e], r * 16 + 16)
                    if not (static and e < 2):
                        dve.wait_ge(xs_turned, n(e) - 2)
                    nc.vector.tensor_scalar(xs_n[:, e % 2, :], xs[:, e, 0:D], xs[:, e, MEAN:MEAN + 1],
                                            xs[:, e, RSTD:RSTD + 1], ALU.subtract, ALU.mult).then_inc(xs_n_ready, 1)
                    dve.wait_ge(xs_n_ready, n(e))
                    nc.vector.scalar_tensor_tensor(xs[:, e, 0:D], b2_bc[:, e, :], xs[:, e, GATE:GATE + 1],
                                                   xs[:, e, 0:D], ALU.mult, ALU.add).then_inc(step, 1)

                def relu(e):
                    dve.wait_ge(l1_done, n(e))
                    if not (static and e < 2):
                        dve.wait_ge(l2_done, n(e) - 2)
                    for f in range(2, KB):
                        last = nc.vector.tensor_scalar(h1T[:, e % 2, f, :], l1_bank[e % 2][1][:, (f - 2) * CAP:(f - 1) * CAP],
                                                       b1T[:, e * KB + f:e * KB + f + 1], 0.0, ALU.add, ALU.max)
                    last.then_inc(relu_dve, 1)

                def finish(e):
                    dve.wait_ge(l2_done, n(e))
                    dve.wait_ge(step, n(e))
                    nc.vector.scalar_tensor_tensor(xs[:, e, 0:D], l2_bank[e % 2][:, :], xs[:, e, GATE:GATE + 1],
                                                   xs[:, e, 0:D], ALU.mult, ALU.add).then_inc(y_ready, 1)

                normalise(0)
                normalise(1)
                for e in range(NE):
                    relu(e)
                    if e + 2 < NE:
                        normalise(e + 2)
                    if e >= 1:
                        finish(e - 1)
                finish(NE - 1)

            b2_added = b2_sum
            dve.wait_ge(b2_loaded, 16)
            dve.wait_ge(b1T_ready, 1)
            round_dve(0, b2_added)

            dve.wait_ge(over_flag, 1)
            more = dve.value_load(flags[0:1, 1:2])
            with dve.If(more != 0):
                with dve.Fori(1, ROUNDS) as r:
                    dve.wait_ge(rows_scattered, r * (16 * NB))
                    nc.vector.tensor_scalar(rank[:, :], rank[:, :], -float(CAP), None, ALU.add).then_inc(round_chain, 1)
                    dve.wait_ge(round_chain, r * 5 - 4)
                    nc.vector.tensor_scalar(over[:, :], rank[:, :], float(CAP), FAR, ALU.is_ge, ALU.mult).then_inc(round_chain, 1)
                    nc.vector.tensor_scalar(slotf[:, :], rank[:, :], 0.0, FAR, ALU.is_lt, ALU.mult).then_inc(round_chain, 1)
                    dve.wait_ge(round_chain, r * 5 - 2)
                    nc.vector.tensor_tensor(over[:, :], over[:, :], slotf[:, :], ALU.add).then_inc(round_chain, 1)
                    dve.wait_ge(round_chain, r * 5 - 1)
                    nc.vector.scalar_tensor_tensor(slotf[:, :], rank[:, :], BASE, over[:, :], ALU.add,
                                                   ALU.add).then_inc(round_chain, 1)
                    dve.wait_ge(round_chain, r * 5)
                    nc.vector.tensor_tensor(slot_i[:, :], slotf[:, :], emin2, ALU.add).then_inc(slots_ready, 1)
                    round_dve(r, b2_added)

        @block.tensor
        def _(pe):
            pe.wait_ge(consts_made, 1)
            pe.wait_ge(keys_made, 1)
            ef = NCH - 128
            for s in range(2):
                nc.tensor.transpose(key_bank[:, s * NCH:s * NCH + 128], key_f[:, s, 0, :], ident[:, :])
                last = nc.tensor.transpose(key_bank[:, s * NCH + 128:(s + 1) * NCH], key_f[0:ef, s, 1, :], ident[0:ef, 0:ef])
            last.then_inc(keys_turned, 1)
            for b in range(NB):
                pe.wait_ge(xn_ready, b + 1)
                if b >= 2:
                    pe.wait_ge(xnT_ready, b - 1)
                for k in range(KB):
                    last = nc.tensor.transpose(turn_bank[b % 2][:, k * BP:(k + 1) * BP], xn[:, b, k * 128:(k + 1) * 128],
                                               ident[0:BP, 0:BP])
                last.then_inc(xn_turned, 1)
            pe.wait_ge(bad_made, 1)
            nc.tensor.matmul(bad_sum, bad[:, :], ones_f[:, 0:1], start=True, stop=True).then_inc(bad_summed, 1)
            pe.wait_ge(small_loaded, 48)
            nc.tensor.transpose(b1_ps, b1_row[:, :], ident[0:NE * KB, 0:NE * KB]).then_inc(b1_turned, 1)

            pe.wait_ge(wa_bc_ready, 1)
            pe.wait_ge(keys_copied, 1)
            pe.wait_ge(xnT_ready, NB)
            for b in range(NB):
                for k in range(KB):
                    last = nc.tensor.matmul(ssrc_ps[:, b:b + 1], xnT[:, k, b * BP:(b + 1) * BP], wa[:, k, 1:2],
                                            start=(k == 0), stop=(k == KB - 1))
            last.then_inc(ssrc_done, 1)
            for lo, hi, to in ((0, 4 * BP, sdst_bank[:, 0:4 * BP]), (4 * BP, N, sdst_last)):
                for k in range(KB):
                    last = nc.tensor.matmul(to, wa_bc[:, k, :], xnT[:, k, lo:hi], start=(k == 0), stop=(k == KB - 1),
                                            skip_group_check=True)
            last.then_inc(sdst_done, 1)

            def project(b):
                if b >= 2:
                    pe.wait_ge(h_copied, b - 1)
                to = h_bank[b % 2][0:BP, :]
                nc.tensor.matmul(to, ones_f[0:1, 0:BP], bw_bc[0:1, :], start=True, stop=False)
                for k in range(KB):
                    last = nc.tensor.matmul(to, xnT[:, k, b * BP:(b + 1) * BP], wg[:, k, :], start=False, stop=(k == KB - 1))
                last.then_inc(h_done, 1)

            for b in range(NB):
                project(b)

            pe.wait_ge(consts_made, 3)
            pe.wait_ge(bad_flag, 1)
            pe.wait_ge(b1T_ready, 1)
            for bank in count_bank:
                nc.tensor.matmul(bank[:, :], zeros_b[:, 0:128], zeros_b[:, :], start=True, stop=False,
                                 skip_group_check=True)

            def count(i, j):
                s = j % RING
                parity, at = (j // GC) % 2, j % GC
                if j % BAT == 0:
                    pe.wait_ge(onehots_made, i * RB + j // BAT + 1)
                lo = (at * STEP - BEFORE) * NB
                cuts = [(lo, min(0, lo + WC), 1 - parity, GW)] if lo < 0 else []
                if lo + WC > GW:
                    cuts.append((max(lo, GW), lo + WC, 1 - parity, -GW))
                cuts.append((max(lo, 0), min(lo + WC, GW), parity, 0))
                last_chunk = isinstance(i, int) and i * RING + j == NCH - 1
                for c0, c1, p, off in cuts:
                    opens = off < 0 and c1 - GW <= STEP * NB
                    if opens:
                        pe.wait_ge(wt_done, i * 2 + j // GC + 1)
                    ins = nc.tensor.matmul(count_bank[p][:, c0 + off:c1 + off], ring[:, s, 0:CH],
                                           ring[:, s, CH + c0 - lo:CH + c1 - lo], start=opens, stop=False,
                                           skip_group_check=True)
                    if off > 0 and c1 - lo <= STEP * NB:
                        ins.then_inc(counts_done, 1)
                if last_chunk:
                    ins.then_inc(counts_done, 1)
                elif j % BAT == BAT - 1:
                    ins.then_inc(onehots_free, 1)

            with pe.Fori(0, NCH // RING) as i:
                for j in range(RING):
                    count(i, j)
            for j in range(NCH % RING):
                count(NCH // RING, j)

            pe.wait_ge(bad_flag, 1)
            outside = pe.value_load(flags[0:1, 0:1])
            with pe.If(outside != 0):
                pe.wait_ge(wt_done, NG + 1)
                with pe.Fori(0, NG) as g:
                    pe.wait_ge(gen_wt, g * 2 + 1)
                    nc.tensor.matmul(count_bank[0][:, :], zeros_b[:, 0:128], zeros_b[:, :], start=True, stop=False,
                                     skip_group_check=True)
                    with pe.Fori(0, NCH) as c:
                        pe.wait_ge(gen_made, g * NCH + c + 1)
                        nc.tensor.matmul(count_bank[0][:, 0:GW], gen_a[:, :], gen_b[:, :], start=False, stop=False,
                                         skip_group_check=True).then_inc(gen_used, 1)
                    nc.tensor.matmul(count_bank[0][:, :], zeros_b[:, 0:128], zeros_b[:, :], start=False, stop=True,
                                     skip_group_check=True).then_inc(gen_counted, 1)
                pe.wait_ge(gen_wt, NG * 2 + 1)

            def aggregate(b):
                pe.wait_ge(wt_done, min(-(-BP * (b + 1) // GN), NG) + 1)
                if b >= 2:
                    pe.wait_ge(agg_used, b - 1)
                pa, pc = agg_bank[b % 2]
                for k in range(NB):
                    lhs = wt[:, k, b * BP:(b + 1) * BP]
                    nc.tensor.matmul(pc[0:BP, 0:256], lhs, hx[:, k, 0:256], start=(k == 0), stop=(k == NB - 1))
                    last = nc.tensor.matmul(pa[0:BP, 0:257], lhs, hx[:, k, 256:513], start=(k == 0), stop=(k == NB - 1))
                last.then_inc(agg_done, 1)

            def turn2(b):
                pe.wait_ge(xn2_ready, b + 1)
                if b >= 2:
                    pe.wait_ge(xn2T_ready, b - 1)
                for k in range(KB):
                    last = nc.tensor.transpose(turn2_bank[b % 2][:, k * BP:(k + 1) * BP], xn[:, b, k * 128:(k + 1) * 128],
                                               ident[0:BP, 0:BP])
                last.then_inc(xn2_turned, 1)

            def route(b):
                pe.wait_ge(xn2T_ready, b + 1)
                for k in range(KB):
                    last = nc.tensor.matmul(logit_ps[:, b, :], xnT[:, k, b * BP:(b + 1) * BP], wr_sb[:, k, :],
                                            start=(k == 0), stop=(k == KB - 1))
                return last

            pe.wait_ge(h_copied, NB)
            pe.wait_ge(b1T_ready, 1)
            for b in range(NB):
                aggregate(b)
                if b >= 1:
                    turn2(b - 1)
                if b >= 2:
                    route(b - 2)
            turn2(NB - 1)
            route(NB - 2)
            route(NB - 1).then_inc(logits_done, 1)

            pe.wait_ge(hot_ready, 1)
            nc.tensor.matmul(rank_ps, lower[:, :], hot[:, :, :], start=True, stop=False, skip_group_check=True)
            for b in range(NB - 1):
                last = nc.tensor.matmul(rank_ps[:, b + 1:NB, :], ones_b[0:BP, 0:BP],
                                        hot[:, b:b + 1, :].to_broadcast([BP, NB - 1 - b, NE]), start=False,
                                        stop=(b == NB - 2), skip_group_check=True)
            last.then_inc(ranks_done, 1)
            pe.wait_ge(over_made, 1)
            nc.tensor.matmul(over_sum, novr[:, :], ones_f[0:BP, 0:1], start=True, stop=True).then_inc(over_summed, 1)

            def round_pe(r):
                static = isinstance(r, int)

                def n(e):
                    return r * NE + e + 1

                def turn(e):
                    pe.wait_ge(xs_n_ready, n(e))
                    if not (static and e < 2):
                        pe.wait_ge(xsT_ready, n(e) - 2)
                    for k in range(KB):
                        last = nc.tensor.transpose(xsT_bank[e % 2][:, k * CAP:(k + 1) * CAP],
                                                   xs_n[:, e % 2, k * 128:(k + 1) * 128], ident[:, :])
                    last.then_inc(xs_turned, 1)

                def layer1(e):
                    pe.wait_ge(xsT_ready, n(e))
                    pe.wait_ge(w_loaded[e], r * 32 + 32)
                    if not (static and e < 2):
                        pe.wait_ge(relu_act, n(e) - 2)
                        pe.wait_ge(relu_dve, n(e) - 2)
                    for f in range(KB):
                        to = l1_bank[e % 2][f // 2][:, (f % 2) * CAP:(f % 2 + 1) * CAP]
                        for k in range(KB):
                            last = nc.tensor.matmul(to,
                                                    w1_sb[:, e % WBUF, k, f * 128:(f + 1) * 128], xsT[:, e % 2, k, :],
                                                    start=(k == 0), stop=(k == KB - 1))
                        if f == 1:
                            last.then_inc(l1_half, 1)
                    last.then_inc(l1_done, 1)

                def layer2(e):
                    pe.wait_ge(relu_act, n(e))
                    pe.wait_ge(relu_dve, n(e))
                    if not (static and e < 2):
                        pe.wait_ge(y_ready, n(e) - 2)
                    for f in range(KB):
                        last = nc.tensor.matmul(l2_bank[e % 2][:, :], h1T[:, e % 2, f, :], w2_sb[:, e % WBUF, f, :],
                                                start=(f == 0), stop=(f == KB - 1))
                    last.then_inc(l2_done, 1)

                turn(0)
                for e in range(NE):
                    if e + 1 < NE:
                        turn(e + 1)
                    layer1(e)
                    if e >= 1:
                        layer2(e - 1)
                layer2(NE - 1)

            pe.wait_ge(over_flag, 1)
            round_pe(0)
            more = pe.value_load(flags[0:1, 1:2])
            with pe.If(more != 0):
                with pe.Fori(1, ROUNDS) as r:
                    round_pe(r)


_INS = ['x', 'src', 'dst', 'L0_gnn_W', 'L0_gnn_b_w', 'L0_gnn_a', 'L0_gnn_b_a', 'L0_ffn_Wr', 'L0_ffn_br', 'L0_ffn_W1',
        'L0_ffn_b1', 'L0_ffn_W2', 'L0_ffn_b2']


def kernel(**inputs):
    import numpy as _np
    import concourse.bacc as _bacc
    from concourse import mybir as _mybir
    from concourse.bass_utils import run_bass_kernel_spmd as _run

    nc = _bacc.Bacc("TRN2", target_bir_lowering=False, num_devices=1)
    arrays, args = {}, []
    for name in _INS:
        a = _np.ascontiguousarray(inputs[name])
        if a.ndim == 0:
            a = a.reshape(1)
        arrays[f"in_{name}_dram"] = a
        args.append(nc.dram_tensor(f"in_{name}_dram", a.shape, _mybir.dt.from_np(a.dtype), kind="ExternalInput").ap())
    args.append(nc.dram_tensor("out_0_dram", (N, D), _mybir.dt.float32, kind="ExternalOutput").ap())
    gnn_ffn(nc, *args)
    r = _run(nc, [arrays], core_ids=[0])
    return r.results[0]["out_0_dram"]
```

```python
from contextlib import ExitStack

import concourse.bass as bass
from concourse import mybir

F32 = mybir.dt.float32
BF16 = mybir.dt.bfloat16
I32 = mybir.dt.int32
U32 = mybir.dt.uint32
ALU = mybir.AluOpType
ACT = mybir.ActivationFunctionType
AX_X = mybir.AxisListType.X

N = 625
D = 512
E = 20000
NE = 8
NB = 5
BP = N // NB
KB = D // 128
EPS = 1e-5
SLOPE = 0.2
MAX_W = 3e38
MIN_DEN = 1e-38

CH = 128
NCH = -(-E // CH)
TAIL = E - (NCH - 1) * CH
HC = (NCH - 1) // 2
STEP = N * CH // E
WIN = 24
BEFORE = 10
GN = 100
GC = GN // STEP
NG = -(-N // GN)
NP = NG * GN
GW = GN * NB
WC = WIN * NB
BAT = 5
NBAT = -(-NCH // BAT)
RB = 16
RING = RB * BAT
OHW = CH + WC

CAP = 128
ROUNDS = -(-N // CAP)
ROW = D + 5
GATE, TOK, MEAN, VAR, RSTD = D, D + 1, D + 2, D + 3, D + 4
HH = D // 2 + 1
FAR = 65536.0
BASE = 4096.0
NO_TOKEN = 1 << 20
WBUF = 4


def gnn_ffn(nc, x, src, dst, w_gnn, b_w, a, b_a, w_r, b_r, w1, b1, w2, b2, out):
    ctx = ExitStack()
    with ctx:
        def sb(name, shape, dt=F32):
            return ctx.enter_context(nc.sbuf_tensor(name, shape, dt))

        def sem(name):
            return ctx.enter_context(nc.semaphore(name))

        rows = sb("rows", [BP, NB, ROW])
        xn = sb("xn", [BP, NB, D])
        xnT = sb("xnT", [128, KB, N])
        hx = sb("hx", [BP, NB, D + 3])
        wexp_xsT = sb("wexp_xsT", [128, NB * NP])
        wexp = wexp_xsT[0:BP, :].rearrange("p (k n) -> p k n", k=NB)
        wt_fill = sb("wt_fill", [128, NB * NP])
        fill = wt_fill[:, 0:ROW]
        a_row = wt_fill[0:1, ROW:ROW + 3 * D].rearrange("p (t n) -> p t n", t=3)
        wt = wt_fill[0:BP, :].rearrange("p (k n) -> p k n", k=NB)
        e2_diag = sb("e2_diag", [BP, 2 * N])
        e2 = e2_diag[:, :].rearrange("p (s n) -> p s n", s=2)
        diag = e2_diag[:, 0:N].rearrange("p (k n) -> p k n", k=NB)
        wg = sb("wg", [128, KB, D + 2])
        a_bc = sb("a_bc", [128, 2, D])
        bw_bc = sb("bw_bc", [128, D + 2])
        ba_bc = sb("ba_bc", [128, 1])
        wr_sb = sb("wr_sb", [128, KB, NE])
        br_bc = sb("br_bc", [BP, NE])
        b1_row = sb("b1_row", [NE * KB, 128])
        b1T = sb("b1T", [128, NE * KB])
        w1_sb = sb("w1_sb", [128, WBUF, KB, D])
        w2_sb = sb("w2_sb", [128, WBUF, KB, D])
        ring_xs = sb("ring_xs", [128, RING * OHW // 2])
        ring = ring_xs[:, :].bitcast(BF16).rearrange("p (s w) -> p s w", s=RING)
        xs = ring_xs[:, 0:NE * ROW].rearrange("p (e r) -> p e r", e=NE)
        b2_bc = ring_xs[:, NE * ROW:NE * (ROW + D)].rearrange("p (e n) -> p e n", e=NE)
        xs_n, xsT, h1T = (wexp_xsT[:, i * 2 * D:(i + 1) * 2 * D] for i in range(3))
        xs_n = xs_n.rearrange("p (s n) -> p s n", s=2)
        xsT = xsT.rearrange("p (s k n) -> p s k n", s=2, k=KB)
        h1T = h1T.rearrange("p (s k n) -> p s k n", s=2, k=KB)

        edge_i = sb("edge_i", [128, 2, 2, CH], I32)
        edge_f = sb("edge_f", [128, 2, 2, CH])
        key_f = sb("key_f", [128, 2, 2, CH])
        hi_f = sb("hi_f", [128, 2, CH])
        keyT = sb("keyT", [128, 2, NCH])
        keyrel = sb("keyrel", [128, NCH])
        key_d = sb("key_d", [128, 2, NCH, 2], BF16)
        clipped = sb("clipped", [128, NCH])
        shift = sb("shift", [128, NCH])
        iota_b = sb("iota_b", [128, CH], BF16)
        iota_g = sb("iota_g", [128, GW])
        gen_ab = edge_f[:, 0, :, :].rearrange("p s c -> p (s c)").bitcast(BF16)
        gen_a = edge_f[:, 1, 0, :].bitcast(BF16)[:, 0:CH]
        gen_b = gen_ab[:, 0:GW]
        ones_f = sb("ones_f", [128, 128])
        ones_b = sb("ones_b", [128, 128], BF16)
        zeros_b = sb("zeros_b", [128, 512], BF16)
        ident = sb("ident", [128, 128])
        lower = sb("lower", [BP, BP], BF16)
        bad = sb("bad", [128, 1])
        flags = sb("flags", [1, 2], I32)
        stats = sb("stats", [BP, 2, 6])
        mv = sb("mv", [BP, NB, 2])
        rstd1 = sb("rstd1", [BP, NB])
        vare = sb("vare", [BP, NB])
        minus_half = sb("minus_half", [BP, 1])
        junk = wexp_xsT[:, 0:D]
        junk_p = wt_fill[:, ROW + 3 * D:ROW + 5 * D].rearrange("p (t n) -> p t n", t=2)
        s_low = sb("s_low", [BP, NB])
        minus_wr = sb("minus_wr", [BP, NE])
        den = sb("den", [BP, 2, 2])
        first_slot = sb("first_slot", [BP, NE])
        raw = sb("raw", [BP, NB, NE])
        lg = sb("lg", [BP, NB, NE])
        mx = sb("mx", [BP, NB])
        cand = sb("cand", [BP, NB, NE])
        emin = sb("emin", [BP, NB])
        hot = sb("hot", [BP, NB, NE], BF16)
        shifted = sb("shifted", [BP, NB, NE])
        gate_e = sb("gate_e", [BP, NB, NE])
        gsum = sb("gsum", [BP, NB])
        prod = sb("prod", [BP, NB, NE])
        rank = sb("rank", [BP, NB])
        over = sb("over", [BP, NB])
        under = sb("under", [BP, NB])
        slot_i = sb("slot_i", [BP, NB], I32)
        novr = sb("novr", [BP, 1])
        xs_dram = nc.dram_tensor("xs_dram", [NE * CAP, ROW], F32, kind="Internal").ap()

        pb = [ctx.enter_context(nc.psum_tensor(f"pb{i}", [128, 512], F32)) for i in range(8)]
        turn_bank = [pb[6], pb[7]]
        key_bank = pb[5]
        spread_bank = [pb[0], pb[1], pb[2]]
        bad_sum = pb[4][0:1, 0:1]
        b1_ps = pb[4][:, 0:NE * KB]
        wr_ps = pb[4][0:BP, 64:64 + NE]
        h_bank = [(pb[0], pb[1]), (pb[2], pb[3])]
        sdst_bank = pb[6]
        sdst_last = pb[7][:, 0:BP]
        count_bank = [pb[4], pb[5], pb[0], pb[1], pb[2], pb[3], pb[4]]
        gen_bank = pb[4]
        agg_bank = [(pb[6], pb[7]), (pb[5], pb[0])]
        turn2_bank = [pb[1], pb[2]]
        logit_bank, rank_bank = pb[3], pb[4]
        over_sum = pb[3][0:1, 64:65]
        xsT_bank = [pb[1], pb[2]]
        l1_bank = [(pb[3], pb[4]), (pb[5], pb[6])]
        l2_bank = [pb[7], pb[0]]

        x_loaded = [sem(f"x_loaded{b}") for b in range(NB)]
        edges_loaded = sem("edges_loaded")
        edges_padded = sem("edges_padded")
        wg_loaded = [sem(f"wg_loaded{k}") for k in range(KB)]
        a_loaded = sem("a_loaded")
        ba_loaded = sem("ba_loaded")
        small_loaded = sem("small_loaded")
        b2_loaded = sem("b2_loaded")
        w_loaded = [sem(f"w_loaded{e}") for e in range(NE)]
        fill_made = sem("fill_made")
        fill_stored = sem("fill_stored")
        pool_chain = sem("pool_chain")
        ones_made = sem("ones_made")
        consts_made = sem("consts_made")
        dve_chain = sem("dve_chain")
        keys_made = sem("keys_made")
        keys_turned = sem("keys_turned")
        keys_copied = sem("keys_copied")
        bad_made = sem("bad_made")
        bad_summed = sem("bad_summed")
        bad_flag = sem("bad_flag")
        xn_ready = sem("xn_ready")
        var_ready = sem("var_ready")
        rstd_ready = sem("rstd_ready")
        xn_turned = sem("xn_turned")
        xnT_ready = sem("xnT_ready")
        sdst_done = sem("sdst_done")
        diag_ready = sem("diag_ready")
        s_low_ready = sem("s_low_ready")
        spread_done = sem("spread_done")
        spread_copied = sem("spread_copied")
        wa_pool = sem("wa_pool")
        wa_ready = sem("wa_ready")
        minus_wr_ready = sem("minus_wr_ready")
        wr_summed = sem("wr_summed")
        x2_ready = sem("x2_ready")
        shift_ready = sem("shift_ready")
        logits_done = sem("logits_done")
        hot_ready = sem("hot_ready")
        ranks_done = sem("ranks_done")
        gates_exp = sem("gates_exp")
        exp_done = sem("exp_done")
        wexp_ready = sem("wexp_ready")
        h_done = sem("h_done")
        h_copied = sem("h_copied")
        onehots_made = sem("onehots_made")
        onehots_free = sem("onehots_free")
        counts_done = sem("counts_done")
        wt_done = sem("wt_done")
        gen_made = sem("gen_made")
        gen_used = sem("gen_used")
        gen_counted = sem("gen_counted")
        gen_wt = sem("gen_wt")
        agg_done = sem("agg_done")
        agg_used = sem("agg_used")
        xn2_turned = sem("xn2_turned")
        xn2T_ready = sem("xn2T_ready")
        b1_turned = sem("b1_turned")
        b1T_ready = sem("b1T_ready")
        over_made = sem("over_made")
        over_summed = sem("over_summed")
        over_flag = sem("over_flag")
        slots_ready = sem("slots_ready")
        rows_scattered = sem("rows_scattered")
        xs_loaded = [sem(f"xs_loaded{e}") for e in range(NE)]
        xs_n_ready = sem("xs_n_ready")
        xs_turned = sem("xs_turned")
        xsT_ready = sem("xsT_ready")
        l1_half = sem("l1_half")
        pool_gate = sem("pool_gate")
        l1_done = sem("l1_done")
        relu_act = sem("relu_act")
        relu_dve = sem("relu_dve")
        l2_done = sem("l2_done")
        b2_sum = sem("b2_sum")
        round_chain = sem("round_chain")
        slot_chain = sem("slot_chain")
        y_ready = sem("y_ready")
        out_written = sem("out_written")

        block = ctx.enter_context(nc.Block())

        def rows_of(t, b, w=D):
            return t[b * BP:(b + 1) * BP, 0:w]

        @block.sync
        def _(sp):
            for b in range(NB):
                sp.dma_start(rows[:, b, 0:D], rows_of(x, b)).then_inc(x_loaded[b], 16)
            for k in range(KB):
                sp.dma_start(wg[:, k, 0:D], w_gnn[k * 128:(k + 1) * 128, :]).then_inc(wg_loaded[k], 16)

            def load_weights(r, e):
                n = r * NE + e
                if not (isinstance(n, int) and n < WBUF):
                    sp.wait_ge(l2_done, n - WBUF + 1)
                sp.dma_start(w1_sb[:, e % WBUF, :, :],
                             w1[e].rearrange("(k p) f -> p k f", p=128)).then_inc(w_loaded[e], 16)
                sp.dma_start(w2_sb[:, e % WBUF, :, :],
                             w2[e].rearrange("(k p) f -> p k f", p=128)).then_inc(w_loaded[e], 16)

            def load_slots(r):
                sp.wait_ge(rows_scattered, (r + 1) * (16 * NB))
                for e in range(NE):
                    sp.dma_start(xs[:, e, :], xs_dram[e * CAP:(e + 1) * CAP, :]).then_inc(xs_loaded[e], 16)

            for e in range(WBUF):
                load_weights(0, e)
            sp.wait_ge(wt_done, NG)
            sp.dma_start(b2_bc, b2.partition_broadcast(128)).then_inc(b2_loaded, 16)
            load_slots(0)
            for e in range(WBUF, NE):
                load_weights(0, e)

            sp.wait_ge(over_flag, 1)
            more = sp.value_load(flags[0:1, 1:2])
            with sp.If(more != 0):
                with sp.Fori(1, ROUNDS) as r:
                    for e in range(WBUF):
                        load_weights(r, e)
                    sp.wait_ge(out_written, r * (16 * NE))
                    load_slots(r)
                    for e in range(WBUF, NE):
                        load_weights(r, e)

        @block.gpsimd
        def _(pool):
            chain = [0]

            def link(ins):
                chain[0] += 1
                ins.then_inc(pool_chain, 1)
                pool.wait_ge(pool_chain, chain[0])

            nc.gpsimd.memset(edge_i[:, 0, :, :], -1).then_inc(edges_padded, 1)
            nc.gpsimd.memset(edge_i[:, 1, :, :], N - 1).then_inc(edges_padded, 1)
            nc.gpsimd.memset(ones_f[:, :], 1.0).then_inc(ones_made, 1)
            link(nc.gpsimd.memset(ident[:, :], 0.0))
            nc.gpsimd.affine_select(out=ident[:, :], in_=ident[:, :], compare_op=ALU.not_equal, fill=1.0,
                                    base=0, pattern=[[-1, 128]], channel_multiplier=1).then_inc(consts_made, 1)
            nc.gpsimd.iota(iota_b[:, :], pattern=[[1, CH]], base=0, channel_multiplier=0,
                           allow_small_or_imprecise_dtypes=True)
            nc.gpsimd.iota(shift[:, :], pattern=[[STEP * NB, NCH]], base=-BEFORE * NB, channel_multiplier=0,
                           allow_small_or_imprecise_dtypes=True).then_inc(consts_made, 1)
            def inv_std(b, which, var, to):
                pool.wait_ge(var_ready, which * NB + b + 1)
                link(nc.gpsimd.tensor_scalar(vare[:, b:b + 1], var, EPS, None, ALU.add))
                nc.gpsimd.tensor_tensor(to, vare[:, b:b + 1], minus_half[:, :], ALU.pow).then_inc(rstd_ready, 1)

            link(nc.gpsimd.memset(minus_half[:, :], -0.5))

            for b in range(NB):
                inv_std(b, 0, mv[:, b, 1:2], rstd1[:, b:b + 1])
            pool.wait_ge(spread_copied, 1)
            pool.wait_ge(wg_loaded[KB - 1], 16)
            for t in range(2):
                nc.gpsimd.tensor_tensor(junk_p[:, t, :], wg[:, KB - 1, 0:D], a_bc[:, t, :], ALU.mult).then_inc(wa_pool, 1)
            nc.gpsimd.memset(zeros_b[:, :], 0.0)
            nc.gpsimd.memset(ones_b[:, :], 1.0).then_inc(consts_made, 1)
            nc.gpsimd.memset(wexp[:, :, N:NP], 0.0)
            nc.gpsimd.memset(hx[:, :, D + 2:D + 3], 1.0).then_inc(consts_made, 1)
            nc.gpsimd.memset(fill[:, :], 0.0).then_inc(pool_chain, 1)
            chain[0] += 1
            pool.wait_ge(pool_chain, chain[0])
            nc.gpsimd.memset(fill[:, TOK:TOK + 1].bitcast(I32), NO_TOKEN).then_inc(fill_made, 1)
            nc.gpsimd.iota(rows[:, :, TOK:TOK + 1].bitcast(I32), pattern=[[BP, NB], [0, 1]], base=0, channel_multiplier=1)
            nc.gpsimd.iota(first_slot[:, :], pattern=[[CAP, NE]], base=-int(BASE), channel_multiplier=0,
                           allow_small_or_imprecise_dtypes=True)
            nc.gpsimd.iota(iota_g[:, :], pattern=[[1, GW]], base=0, channel_multiplier=0,
                           allow_small_or_imprecise_dtypes=True)
            link(nc.gpsimd.memset(lower[:, :], 1.0))
            nc.gpsimd.affine_select(out=lower[:, :], in_=lower[:, :], compare_op=ALU.is_gt, fill=0.0,
                                    base=0, pattern=[[1, BP]], channel_multiplier=-1).then_inc(consts_made, 1)

            for k in range(NB):
                pool.wait_ge(h_copied, k + 1)
                nc.gpsimd.tensor_scalar(s_low[:, k:k + 1], hx[:, k, D + 1:D + 2], SLOPE, None,
                                        ALU.mult).then_inc(s_low_ready, 1)
            slot_bound = pool.to_reg(NE * CAP - 1)
            token_bound = pool.to_reg(N - 1)

            def scatter_rows(r, b):
                pool.wait_ge(slots_ready, r * NB + b + 1)
                pool.sem_inc(pool_gate, 1)
                pool.indirect_dma_start(
                    out=xs_dram, out_offset=bass.IndirectOffsetOnAxis(ap=slot_i[:, b:b + 1].bitcast(U32), axis=0),
                    in_=rows[:, b, :], in_offset=None, bounds_check=slot_bound,
                    oob_is_err=False).then_inc(rows_scattered, 16)

            def scatter_out(r):
                for e in range(NE):
                    pool.wait_ge(y_ready, r * NE + e + 1)
                    pool.sem_inc(pool_gate, 1)
                    pool.indirect_dma_start(
                        out=out, out_offset=bass.IndirectOffsetOnAxis(ap=xs[:, e, TOK:TOK + 1].bitcast(U32), axis=0),
                        in_=xs[:, e, 0:D], in_offset=None, bounds_check=token_bound,
                        oob_is_err=False).then_inc(out_written, 16)

            pool.wait_ge(fill_stored, 16)
            inv_std(0, 1, rows[:, 0, VAR:VAR + 1], rows[:, 0, RSTD:RSTD + 1])
            for b in range(NB):
                if b + 1 < NB:
                    inv_std(b + 1, 1, rows[:, b + 1, VAR:VAR + 1], rows[:, b + 1, RSTD:RSTD + 1])
                scatter_rows(0, b)
            scatter_out(0)
            pool.wait_ge(out_written, 16 * NE)
            pool.wait_ge(over_flag, 1)
            more = pool.value_load(flags[0:1, 1:2])
            with pool.If(more != 0):
                with pool.Fori(1, ROUNDS) as r:
                    for b in range(NB):
                        scatter_rows(r, b)
                    scatter_out(r)
                    pool.wait_ge(out_written, r * (16 * NE) + 16 * NE)
                nc.gpsimd.engine_nop()

        @block.scalar
        def _(act):
            act.dma_start(a_row[:, 0:2, :], a.rearrange("(o t n) -> o t n", o=1, t=2)).then_inc(a_loaded, 16)
            act.dma_start(a_row[:, 2, :], b_w.unsqueeze(0)).then_inc(a_loaded, 16)
            act.wait_ge(edges_padded, 2)
            for s, t in enumerate((src, dst)):
                act.dma_start(edge_i[0:HC, s, :, :],
                              t[0:2 * HC * CH].rearrange("(h p c) -> p h c", p=HC, c=CH)).then_inc(edges_loaded, 16)
                act.dma_start(edge_i[HC:HC + 1, s, 1, 0:TAIL], t[2 * HC * CH:E].unsqueeze(0)).then_inc(edges_loaded, 16)
            act.dma_start(ba_bc[:, :], b_a.partition_broadcast(128)).then_inc(ba_loaded, 16)
            act.dma_start(wr_sb[:, :, :], w_r.rearrange("(k p) n -> p k n", p=128)).then_inc(small_loaded, 16)
            act.dma_start(br_bc[:, :], b_r.partition_broadcast(BP)).then_inc(small_loaded, 16)
            act.dma_start(b1_row[:, :], b1.rearrange("e (k p) -> (e k) p", p=128)).then_inc(small_loaded, 16)

            act.wait_ge(spread_done, 1)
            for t in range(2):
                nc.scalar.copy(a_bc[:, t, :], spread_bank[t][:, :])
            nc.scalar.copy(bw_bc[:, 0:D], spread_bank[2][:, :]).then_inc(spread_copied, 1)
            for b in range(NB):
                act.wait_ge(xn_turned, b + 1)
                nc.scalar.copy(xnT[:, :, b * BP:(b + 1) * BP],
                               turn_bank[b % 2][:, 0:KB * BP].rearrange("p (k n) -> p k n", k=KB)).then_inc(xnT_ready, 1)
            for t in range(2):
                act.wait_ge(wa_pool, t + 1)
                nc.scalar.activation(junk_p[:, t, :], junk_p[:, t, :], ACT.Copy,
                                     accum_out=wg[:, KB - 1, D + t:D + t + 1]).then_inc(wa_ready, 1)
            act.wait_ge(keys_turned, 1)
            nc.scalar.copy(keyT[:, :, :], key_bank[:, 0:2 * NCH].rearrange("p (s c) -> p s c", s=2)).then_inc(keys_copied, 1)
            act.wait_ge(b1_turned, 1)
            nc.scalar.copy(b1T[:, :], b1_ps).then_inc(b1T_ready, 1)
            act.wait_ge(fill_made, 1)
            act.dma_start(xs_dram.rearrange("(e p) r -> p e r", p=CAP),
                          fill[:, :].unsqueeze(1).to_broadcast([128, NE, ROW])).then_inc(fill_stored, 16)
            act.wait_ge(sdst_done, 1)
            n0 = 4 * BP
            for k in range(NB):
                act.wait_ge(s_low_ready, k + 1)
                nc.scalar.activation(wexp[:, k, 0:n0], sdst_bank[0:BP, 0:n0], ACT.Exp, bias=hx[:, k, D + 1:D + 2])
                nc.scalar.activation(wexp[:, k, n0:N], sdst_last[0:BP, :], ACT.Exp,
                                     bias=hx[:, k, D + 1:D + 2]).then_inc(exp_done, 1)
                if k >= 2:
                    act.wait_ge(wexp_ready, k - 1)
                nc.scalar.activation(e2[:, k % 2, 0:n0], sdst_bank[0:BP, 0:n0], ACT.Exp,
                                     bias=s_low[:, k:k + 1], scale=SLOPE)
                nc.scalar.activation(e2[:, k % 2, n0:N], sdst_last[0:BP, :], ACT.Exp,
                                     bias=s_low[:, k:k + 1], scale=SLOPE).then_inc(exp_done, 1)

            def copy_x2T(b):
                act.wait_ge(xn2_turned, b + 1)
                nc.scalar.copy(xnT[:, :, b * BP:(b + 1) * BP],
                               turn2_bank[b % 2][:, 0:KB * BP].rearrange("p (k n) -> p k n", k=KB)).then_inc(xn2T_ready, 1)

            def gate(b):
                act.wait_ge(shift_ready, b + 1)
                nc.scalar.activation(gate_e[:, b, :], shifted[:, b, :], ACT.Exp,
                                     accum_out=gsum[:, b:b + 1]).then_inc(gates_exp, 1)

            copy_x2T(0)
            for b in range(NB):
                if b + 1 < NB:
                    copy_x2T(b + 1)
                gate(b)

            def round_act(r):
                for e in range(NE):
                    def n(back=0):
                        return r * NE + e + 1 - back
                    act.wait_ge(xs_turned, n())
                    if not (isinstance(r, int) and e < 2):
                        act.wait_ge(l1_done, n(2))
                    nc.scalar.copy(xsT[:, e % 2, :, :],
                                   xsT_bank[e % 2][:, :].rearrange("p (k n) -> p k n", k=KB)).then_inc(xsT_ready, 1)
                    if e >= 1:
                        relu(r, e - 1)
                relu(r, NE - 1)

            def relu(r, e):
                act.wait_ge(l1_half, r * NE + e + 1)
                if not (isinstance(r, int) and e < 2):
                    act.wait_ge(l2_done, r * NE + e - 1)
                for f in range(2):
                    last = nc.scalar.activation(h1T[:, e % 2, f, :], l1_bank[e % 2][0][:, f * CAP:(f + 1) * CAP], ACT.Relu,
                                                bias=b1T[:, e * KB + f:e * KB + f + 1])
                last.then_inc(relu_act, 1)

            round_act(0)
            act.wait_ge(over_flag, 1)
            more = act.value_load(flags[0:1, 1:2])
            with act.If(more != 0):
                with act.Fori(1, ROUNDS) as r:
                    round_act(r)

        @block.vector
        def _(dve):
            chain = [0]

            def link(ins):
                chain[0] += 1
                ins.then_inc(dve_chain, 1)
                dve.wait_ge(dve_chain, chain[0])

            def make_keys():
                live = slice(0, HC + 1)
                dve.wait_ge(edges_loaded, 4 * 16)
                link(nc.vector.tensor_copy(edge_f[live, :, :, :], edge_i[live, :, :, :]))
                srcf, dstf, hi = edge_f[live, 0, :, :], edge_f[live, 1, :, :], hi_f[live, :, :]
                link(nc.vector.tensor_scalar(hi, srcf, float(BP), None, ALU.is_ge))
                for k in range(2, NB):
                    link(nc.vector.scalar_tensor_tensor(hi, srcf, float(BP * k), hi, ALU.is_ge, ALU.add))
                nc.vector.scalar_tensor_tensor(key_f[live, 0, :, :], hi, -float(BP), srcf, ALU.mult, ALU.add)
                nc.vector.scalar_tensor_tensor(key_f[live, 1, :, :], dstf, float(NB), hi, ALU.mult,
                                               ALU.add).then_inc(keys_made, 1)

            def dot_a(row, t, to):
                link(nc.vector.tensor_tensor_reduce(out=junk[:, :], in0=row, in1=a_bc[:, t, :], scale=1.0, scalar=0.0,
                                                    op0=ALU.mult, op1=ALU.add, accum_out=to))

            def normalise_block(b):
                dve.wait_ge(rstd_ready, b + 1)
                nc.vector.tensor_scalar(xn[:, b, :], rows[:, b, 0:D], mv[:, b, 0:1], rstd1[:, b:b + 1], ALU.subtract,
                                        ALU.mult).then_inc(xn_ready, 1)

            for b in range(NB):
                dve.wait_ge(x_loaded[b], 16)
                link(nc.vector.bn_stats(stats[:, b % 2, :], rows[:, b, 0:D]))
                nc.vector.bn_aggr(mv[:, b, :], stats[:, b % 2, :]).then_inc(var_ready, 1)
                if b >= 1:
                    normalise_block(b - 1)
            normalise_block(NB - 1)
            dve.wait_ge(spread_copied, 1)
            for k in range(KB - 1):
                dve.wait_ge(wg_loaded[k], 16)
                for t in range(2):
                    dot_a(wg[:, k, 0:D], t, wg[:, k, D + t:D + t + 1])
            dve.sem_inc(wa_ready, 1)
            make_keys()
            for t in range(2):
                dot_a(bw_bc[:, 0:D], t, bw_bc[:, D + t:D + t + 1])
            dve.wait_ge(ba_loaded, 16)
            link(nc.vector.tensor_tensor(bw_bc[:, D + 1:D + 2], bw_bc[:, D + 1:D + 2], ba_bc[:, :], ALU.add))
            dve.wait_ge(keys_copied, 1)
            dve.wait_ge(consts_made, 2)
            link(nc.vector.tensor_tensor(keyrel[:, :], keyT[:, 1, :], shift[:, :], ALU.subtract))
            for s, t in enumerate((keyT[:, 0, :], keyrel[:, :])):
                link(nc.vector.tensor_copy(key_d[:, s, :, :], t.unsqueeze(2).to_broadcast([128, NCH, 2])))

            def onehots(q):
                n = min(BAT, NCH - q * BAT)
                if q >= RB:
                    dve.wait_ge(onehots_free, q - RB + 1)
                to = ring[:, (q % RB) * BAT:(q % RB) * BAT + n, :]
                for s, c0, w in ((0, 0, CH), (1, CH, WC)):
                    shape = [128, n, w // 2, 2]
                    ins = nc.vector.tensor_tensor(
                        to[:, :, c0:c0 + w].rearrange("p c (w t) -> p c w t", t=2),
                        iota_b[:, 0:w].rearrange("p (w t) -> p w t", t=2).unsqueeze(1).to_broadcast(shape),
                        key_d[:, s, q * BAT:q * BAT + n, :].unsqueeze(2).to_broadcast(shape), ALU.is_equal)
                ins.then_inc(onehots_made, 1)

            def weigh(g, ready, ps, done):
                at = bass.ds(g * GN, GN)
                dve.wait_ge(*ready)
                nc.vector.scalar_tensor_tensor(wt[:, :, at], wexp[:, :, at], MAX_W,
                                               ps[0:BP, 0:GW].rearrange("p (n k) -> p k n", k=NB),
                                               ALU.min, ALU.mult).then_inc(done, 1)

            def weigh_band(g):
                weigh(g, (counts_done, g + 1), count_bank[g], wt_done)

            def whole_exp(k):
                dve.wait_ge(exp_done, 2 * (k + 1))
                nc.vector.tensor_tensor(wexp[:, k, 0:N], wexp[:, k, 0:N], e2[:, k % 2, :],
                                        ALU.max).then_inc(wexp_ready, 1)

            def keep_h(k):
                dve.wait_ge(h_done, k + 1)
                for t in range(2):
                    at = slice(t * HH, (t + 1) * HH)
                    last = nc.vector.tensor_tensor(hx[:, k, at], h_bank[k % 2][t][0:BP, 0:HH], bw_bc[0:BP, at], ALU.add)
                last.then_inc(h_copied, 1)

            KEEP = {2: 0, 7: 1, 12: 2}
            for q in range(RB):
                onehots(q)
                if q in KEEP:
                    keep_h(KEEP[q])
                if q == 0:
                    link(nc.vector.tensor_scalar(clipped[:, :], keyrel[:, :], 0.0, float(WC - 1), ALU.max, ALU.min))
                    link(nc.vector.tensor_tensor(clipped[:, :], clipped[:, :], keyrel[:, :], ALU.not_equal))
                    nc.vector.tensor_reduce(bad[:, :], clipped[:, :], AX_X, ALU.add).then_inc(bad_made, 1)
                if q == RB - 1:
                    dve.wait_ge(bad_summed, 1)
                    dve.wait_ge(wr_summed, 1)
                    nc.vector.tensor_copy(flags[0:1, 0:1], bad_sum).then_inc(bad_flag, 1)
                    nc.vector.tensor_scalar(minus_wr[:, :], wr_ps, -1.0, None, ALU.mult).then_inc(minus_wr_ready, 1)
            for k in range(NB):
                if k >= 3:
                    keep_h(k)
                dve.wait_ge(h_copied, k + 1)
                nc.vector.tensor_scalar(diag[:, k, :], ident[0:BP, 0:BP], hx[:, k, D:D + 1], None,
                                        ALU.mult).then_inc(diag_ready, 1)
            q = RB
            for k in range(NB):
                for _ in range(2):
                    onehots(q)
                    q += 1
                whole_exp(k)
            dve.wait_ge(consts_made, 4)
            dve.wait_ge(fill_stored, 16)
            dve.wait_ge(wexp_ready, NB)
            for g in range(NG - 1):
                weigh_band(g)
                if q < NBAT:
                    onehots(q)
                    q += 1
            weigh_band(NG - 1)

            dve.wait_ge(bad_flag, 1)
            outside = dve.value_load(flags[0:1, 0:1])
            with dve.If(outside != 0):
                dve.wait_ge(wt_done, NG)
                dve.wait_ge(consts_made, 5)
                dve.sem_inc(gen_used, 1)
                dve.sem_inc(gen_wt, 1)
                with dve.Fori(0, NG) as g:
                    with dve.Fori(0, NCH) as c:
                        dve.wait_ge(gen_used, g * NCH + c + 1)
                        nc.vector.tensor_scalar(gen_a[:, :], iota_b[:, :], keyT[:, 0, bass.ds(c, 1)], None, ALU.is_equal)
                        nc.vector.tensor_scalar(gen_b[:, :], iota_g[:, :], keyT[:, 1, bass.ds(c, 1)], None,
                                                ALU.is_equal).then_inc(gen_made, 1)
                    weigh(g, (gen_counted, g + 1), gen_bank, gen_wt)
                    nc.vector.tensor_scalar(keyT[:, 1, :], keyT[:, 1, :], -float(GW), None, ALU.add).then_inc(gen_wt, 1)
                    dve.wait_ge(gen_wt, g * 2 + 3)

            def add_gnn(b):
                pa, pc = agg_bank[b % 2]
                dve.wait_ge(agg_done, b + 1)
                link(nc.vector.tensor_scalar(den[:, b % 2, 0:1], pc[0:BP, HH:HH + 1], MIN_DEN, None, ALU.max))
                link(nc.vector.reciprocal(den[:, b % 2, 1:2], den[:, b % 2, 0:1]))
                nc.vector.scalar_tensor_tensor(rows[:, b, 0:HH], pa[0:BP, 0:HH], den[:, b % 2, 1:2], rows[:, b, 0:HH],
                                               ALU.mult, ALU.add)
                nc.vector.scalar_tensor_tensor(rows[:, b, HH:D], pc[0:BP, 0:D - HH], den[:, b % 2, 1:2],
                                               rows[:, b, HH:D], ALU.mult, ALU.add).then_inc(x2_ready, 1)
                dve.wait_ge(x2_ready, b + 1)
                link(nc.vector.bn_stats(stats[:, b % 2, :], rows[:, b, 0:D]))
                nc.vector.bn_aggr(rows[:, b, MEAN:MEAN + 2], stats[:, b % 2, :]).then_inc(var_ready, 1)

            def choose(b):
                dve.wait_ge(logits_done, b + 1)
                dve.wait_ge(var_ready, NB + b + 1)
                link(nc.vector.scalar_tensor_tensor(raw[:, b, :], minus_wr[:, :], rows[:, b, MEAN:MEAN + 1],
                                                    logit_bank[0:BP, b * NE:(b + 1) * NE], ALU.mult, ALU.add))
                dve.wait_ge(rstd_ready, NB + b + 1)
                link(nc.vector.scalar_tensor_tensor(lg[:, b, :], raw[:, b, :], rows[:, b, RSTD:RSTD + 1], br_bc[:, :],
                                                    ALU.mult, ALU.add))
                link(nc.vector.tensor_reduce(mx[:, b:b + 1], lg[:, b, :], AX_X, ALU.max))
                link(nc.vector.scalar_tensor_tensor(cand[:, b, :], lg[:, b, :], mx[:, b:b + 1], first_slot[:, :],
                                                    ALU.is_equal, ALU.mult))
                link(nc.vector.tensor_reduce(emin[:, b:b + 1], cand[:, b, :], AX_X, ALU.min))
                nc.vector.tensor_scalar(hot[:, b, :], cand[:, b, :], emin[:, b:b + 1], None,
                                        ALU.is_equal).then_inc(hot_ready, 1)
                nc.vector.tensor_scalar(shifted[:, b, :], lg[:, b, :], mx[:, b:b + 1], None,
                                        ALU.subtract).then_inc(shift_ready, 1)

            def find_slot(b):
                dve.wait_ge(gates_exp, b + 1)
                nc.vector.reciprocal(rows[:, b, GATE:GATE + 1], gsum[:, b:b + 1])
                dve.wait_ge(hot_ready, b + 1)
                dve.wait_ge(ranks_done, b + 1)
                link(nc.vector.tensor_tensor_reduce(out=prod[:, b, :], in0=rank_bank[0:BP, b * NE:(b + 1) * NE],
                                                    in1=hot[:, b, :], scale=1.0, scalar=BASE, op0=ALU.mult, op1=ALU.add,
                                                    accum_out=rank[:, b:b + 1]))
                link(nc.vector.tensor_scalar(over[:, b:b + 1], rank[:, b:b + 1], BASE + CAP, FAR, ALU.is_ge, ALU.mult))
                nc.vector.scalar_tensor_tensor(slot_i[:, b:b + 1], rank[:, b:b + 1], emin[:, b:b + 1], over[:, b:b + 1],
                                               ALU.add, ALU.add).then_inc(slots_ready, 1)

            dve.wait_ge(small_loaded, 48)
            dve.wait_ge(consts_made, 5)
            dve.wait_ge(minus_wr_ready, 1)
            for b in range(NB):
                add_gnn(b)
                if b >= 1:
                    find_slot(b - 1)
                choose(b)
            find_slot(NB - 1)
            nc.vector.tensor_reduce(novr[:, :], over[:, :], AX_X, ALU.add).then_inc(over_made, 1)
            dve.wait_ge(over_summed, 1)
            nc.vector.tensor_copy(flags[0:1, 1:2], over_sum).then_inc(over_flag, 1)

            def round_dve(r, step):
                static = isinstance(r, int)

                def n(e):
                    return r * NE + e + 1

                def normalise(e):
                    dve.wait_ge(xs_loaded[e], r * 16 + 16)
                    if not (static and e < 2):
                        dve.wait_ge(xs_turned, n(e) - 2)
                    nc.vector.tensor_scalar(xs_n[:, e % 2, :], xs[:, e, 0:D], xs[:, e, MEAN:MEAN + 1],
                                            xs[:, e, RSTD:RSTD + 1], ALU.subtract, ALU.mult).then_inc(xs_n_ready, 1)
                    dve.wait_ge(xs_n_ready, n(e))
                    nc.vector.scalar_tensor_tensor(xs[:, e, 0:D], b2_bc[:, e, :], xs[:, e, GATE:GATE + 1],
                                                   xs[:, e, 0:D], ALU.mult, ALU.add).then_inc(step, 1)

                def relu(e):
                    dve.wait_ge(l1_done, n(e))
                    if not (static and e < 2):
                        dve.wait_ge(l2_done, n(e) - 2)
                    for f in range(2, KB):
                        last = nc.vector.tensor_scalar(h1T[:, e % 2, f, :], l1_bank[e % 2][1][:, (f - 2) * CAP:(f - 1) * CAP],
                                                       b1T[:, e * KB + f:e * KB + f + 1], 0.0, ALU.add, ALU.max)
                    last.then_inc(relu_dve, 1)

                def finish(e):
                    dve.wait_ge(l2_done, n(e))
                    dve.wait_ge(step, n(e))
                    nc.vector.scalar_tensor_tensor(xs[:, e, 0:D], l2_bank[e % 2][:, :], xs[:, e, GATE:GATE + 1],
                                                   xs[:, e, 0:D], ALU.mult, ALU.add).then_inc(y_ready, 1)

                normalise(0)
                normalise(1)
                for e in range(NE):
                    relu(e)
                    if e + 2 < NE:
                        normalise(e + 2)
                    if e >= 1:
                        finish(e - 1)
                finish(NE - 1)

            b2_added = b2_sum
            dve.wait_ge(b2_loaded, 16)
            dve.wait_ge(b1T_ready, 1)
            round_dve(0, b2_added)

            dve.wait_ge(over_flag, 1)
            more = dve.value_load(flags[0:1, 1:2])
            with dve.If(more != 0):
                with dve.Fori(1, ROUNDS) as r:
                    dve.wait_ge(rows_scattered, r * (16 * NB))
                    nc.vector.tensor_scalar(rank[:, :], rank[:, :], -float(CAP), None, ALU.add).then_inc(round_chain, 1)
                    dve.wait_ge(round_chain, r * 4 - 3)
                    nc.vector.tensor_scalar(over[:, :], rank[:, :], BASE + CAP, FAR, ALU.is_ge, ALU.mult).then_inc(round_chain, 1)
                    nc.vector.scalar_tensor_tensor(under[:, :], rank[:, :], BASE, emin[:, :], ALU.is_lt,
                                                   ALU.mult).then_inc(round_chain, 1)
                    dve.wait_ge(round_chain, r * 4 - 1)
                    nc.vector.scalar_tensor_tensor(over[:, :], under[:, :], -FAR, over[:, :], ALU.mult,
                                                   ALU.add).then_inc(round_chain, 1)
                    dve.wait_ge(round_chain, r * 4)
                    nc.vector.tensor_tensor(over[:, :], over[:, :], emin[:, :], ALU.add).then_inc(slot_chain, 1)
                    dve.wait_ge(slot_chain, r)
                    nc.vector.tensor_tensor(slot_i[:, :], over[:, :], rank[:, :], ALU.add).then_inc(slots_ready, NB)
                    round_dve(r, b2_added)

        @block.tensor
        def _(pe):
            pe.wait_ge(ones_made, 1)
            pe.wait_ge(a_loaded, 32)
            for t in range(3):
                last = nc.tensor.matmul(spread_bank[t][:, :], ones_f[0:1, :], a_row[:, t, :], start=True, stop=True)
            last.then_inc(spread_done, 1)
            pe.wait_ge(consts_made, 1)
            for b in range(NB):
                pe.wait_ge(xn_ready, b + 1)
                if b >= 2:
                    pe.wait_ge(xnT_ready, b - 1)
                for k in range(KB):
                    last = nc.tensor.transpose(turn_bank[b % 2][:, k * BP:(k + 1) * BP], xn[:, b, k * 128:(k + 1) * 128],
                                               ident[0:BP, 0:BP])
                last.then_inc(xn_turned, 1)
            pe.wait_ge(small_loaded, 48)
            nc.tensor.transpose(b1_ps, b1_row[:, :], ident[0:NE * KB, 0:NE * KB]).then_inc(b1_turned, 1)
            def project(b):
                if b >= 2:
                    pe.wait_ge(h_copied, b - 1)
                for t in range(2):
                    to, at = h_bank[b % 2][t][0:BP, 0:HH], slice(t * HH, (t + 1) * HH)
                    for k in range(KB):
                        last = nc.tensor.matmul(to, xnT[:, k, b * BP:(b + 1) * BP], wg[:, k, at], start=(k == 0),
                                                stop=(k == KB - 1))
                last.then_inc(h_done, 1)

            pe.wait_ge(spread_copied, 1)
            pe.wait_ge(wa_ready, 3)
            for b in range(NB):
                pe.wait_ge(xnT_ready, b + 1)
                project(b)
                if b == 0:
                    pe.wait_ge(keys_made, 1)
                    for s in range(2):
                        for h in range(2):
                            last = nc.tensor.transpose(key_bank[:, s * NCH + h * HC:s * NCH + h * HC + HC + h],
                                                       key_f[0:HC + h, s, h, :], ident[0:HC + h, 0:HC + h])
                    last.then_inc(keys_turned, 1)
            pe.wait_ge(b1T_ready, 1)
            pe.wait_ge(bad_made, 1)
            nc.tensor.matmul(bad_sum, bad[:, :], ones_f[:, 0:1], start=True, stop=True).then_inc(bad_summed, 1)
            for k in range(KB):
                last = nc.tensor.matmul(wr_ps, ones_f[:, 0:BP], wr_sb[:, k, :], start=(k == 0), stop=(k == KB - 1),
                                        skip_group_check=True)
            last.then_inc(wr_summed, 1)

            def opens_bank(g):
                if g < 2:
                    pe.wait_ge(bad_flag, 1)
                    pe.wait_ge(minus_wr_ready, 1)
                    pe.wait_ge(keys_copied, 1)
                elif g < NG - 1:
                    pe.wait_ge(h_copied, NB)
                else:
                    pe.wait_ge(wt_done, 1)

            opened = set()

            def count(c):
                s, q = c % RING, c // BAT
                if c % BAT == 0:
                    pe.wait_ge(onehots_made, q + 1)
                lo = (c * STEP - BEFORE) * NB
                hi = lo + WC
                g0, g1 = max(lo, 0) // GW, min(hi - 1, N * NB - 1) // GW
                for g in range(g0, g1 + 1):
                    c0, c1 = max(lo, g * GW, 0), min(hi, (g + 1) * GW, N * NB)
                    if g not in opened:
                        opens_bank(g)
                    ins = nc.tensor.matmul(count_bank[g][:, c0 - g * GW:c1 - g * GW], ring[:, s, 0:CH],
                                           ring[:, s, CH + c0 - lo:CH + c1 - lo], start=g not in opened, stop=False,
                                           skip_group_check=True)
                    opened.add(g)
                    if g == g0 and (c == NCH - 1 or (lo + STEP * NB) // GW > g0 >= 0 and lo >= 0):
                        ins.then_inc(counts_done, 1)
                        if g1 == g0 and c % BAT == BAT - 1:
                            pe.sem_inc(onehots_free, 1)
                    elif g == g1 and c % BAT == BAT - 1:
                        ins.then_inc(onehots_free, 1)

            def repeat_sdst():
                for k in range(NB):
                    pe.wait_ge(diag_ready, k + 1)
                    to = sdst_bank[0:BP, k * BP:(k + 1) * BP] if k < 4 else sdst_last[0:BP, :]
                    last = nc.tensor.matmul(to, ones_f[0:BP, 0:BP], diag[:, k, :], start=True, stop=True)
                last.then_inc(sdst_done, 1)

            for c in range(NCH):
                if c == BAT:
                    repeat_sdst()
                count(c)

            pe.wait_ge(bad_flag, 1)
            outside = pe.value_load(flags[0:1, 0:1])
            with pe.If(outside != 0):
                pe.wait_ge(wt_done, NG)
                with pe.Fori(0, NG) as g:
                    pe.wait_ge(gen_wt, g * 2 + 1)
                    nc.tensor.matmul(gen_bank[:, :], zeros_b[:, 0:128], zeros_b[:, :], start=True, stop=False,
                                     skip_group_check=True)
                    with pe.Fori(0, NCH) as c:
                        pe.wait_ge(gen_made, g * NCH + c + 1)
                        nc.tensor.matmul(gen_bank[:, 0:GW], gen_a[:, :], gen_b[:, :], start=False, stop=False,
                                         skip_group_check=True).then_inc(gen_used, 1)
                    nc.tensor.matmul(gen_bank[:, :], zeros_b[:, 0:128], zeros_b[:, :], start=False, stop=True,
                                     skip_group_check=True).then_inc(gen_counted, 1)
                pe.wait_ge(gen_wt, NG * 2 + 1)

            def aggregate(b, k):
                if k == 0:
                    pe.wait_ge(wt_done, min(-(-BP * (b + 1) // GN), NG))
                    if b >= 2:
                        pe.wait_ge(x2_ready, b - 1)
                pa, pc = agg_bank[b % 2]
                lhs = wt[:, k, b * BP:(b + 1) * BP]
                nc.tensor.matmul(pa[0:BP, 0:HH], lhs, hx[:, k, 0:HH], start=(k == 0), stop=(k == NB - 1))
                last = nc.tensor.matmul(pc[0:BP, 0:HH + 1], lhs, hx[:, k, HH:2 * HH + 1], start=(k == 0), stop=(k == NB - 1))
                if k == NB - 1:
                    last.then_inc(agg_done, 1)

            def turn2(b):
                pe.wait_ge(x2_ready, b + 1)
                if b == 0:
                    pe.wait_ge(wt_done, NG)
                if b >= 2:
                    pe.wait_ge(xn2T_ready, b - 1)
                for k in range(KB):
                    last = nc.tensor.transpose(turn2_bank[b % 2][:, k * BP:(k + 1) * BP], rows[:, b, k * 128:(k + 1) * 128],
                                               ident[0:BP, 0:BP])
                last.then_inc(xn2_turned, 1)

            def route(b):
                pe.wait_ge(xn2T_ready, b + 1)
                if b >= 1:
                    pe.wait_ge(hot_ready, b)
                for k in range(KB):
                    last = nc.tensor.matmul(logit_bank[0:BP, b * NE:(b + 1) * NE], xnT[:, k, b * BP:(b + 1) * BP],
                                            wr_sb[:, k, :], start=(k == 0), stop=(k == KB - 1))
                last.then_inc(logits_done, 1)

            def order(b):
                pe.wait_ge(hot_ready, b + 1)
                if b >= 1:
                    pe.wait_ge(slots_ready, b)
                to = rank_bank[0:BP, b * NE:(b + 1) * NE]
                for t in range(b):
                    nc.tensor.matmul(to, ones_b[0:BP, 0:BP], hot[:, t, :], start=(t == 0), stop=False)
                nc.tensor.matmul(to, lower[:, :], hot[:, b, :], start=(b == 0), stop=True).then_inc(ranks_done, 1)

            pe.wait_ge(consts_made, 5)
            for b in range(NB):
                for k in range(NB):
                    if b >= 1 and k == 2:
                        turn2(b - 1)
                    if b >= 1 and k == 4:
                        route(b - 1)
                    if b >= 2 and k == 1:
                        order(b - 2)
                    aggregate(b, k)
            order(NB - 2)
            turn2(NB - 1)
            route(NB - 1)
            order(NB - 1)
            pe.wait_ge(over_made, 1)
            nc.tensor.matmul(over_sum, novr[:, :], ones_f[0:BP, 0:1], start=True, stop=True).then_inc(over_summed, 1)

            def round_pe(r):
                static = isinstance(r, int)

                def n(e):
                    return r * NE + e + 1

                def turn(e):
                    pe.wait_ge(xs_n_ready, n(e))
                    if not (static and e < 2):
                        pe.wait_ge(xsT_ready, n(e) - 2)
                    for k in range(KB):
                        last = nc.tensor.transpose(xsT_bank[e % 2][:, k * CAP:(k + 1) * CAP],
                                                   xs_n[:, e % 2, k * 128:(k + 1) * 128], ident[:, :])
                    last.then_inc(xs_turned, 1)

                def layer1(e):
                    pe.wait_ge(xsT_ready, n(e))
                    pe.wait_ge(w_loaded[e], r * 32 + 32)
                    if not (static and e < 2):
                        pe.wait_ge(relu_act, n(e) - 2)
                        pe.wait_ge(relu_dve, n(e) - 2)
                    for f in range(KB):
                        to = l1_bank[e % 2][f // 2][:, (f % 2) * CAP:(f % 2 + 1) * CAP]
                        for k in range(KB):
                            last = nc.tensor.matmul(to,
                                                    w1_sb[:, e % WBUF, k, f * 128:(f + 1) * 128], xsT[:, e % 2, k, :],
                                                    start=(k == 0), stop=(k == KB - 1))
                        if f == 1:
                            last.then_inc(l1_half, 1)
                    last.then_inc(l1_done, 1)

                def layer2(e):
                    pe.wait_ge(relu_act, n(e))
                    pe.wait_ge(relu_dve, n(e))
                    if not (static and e < 2):
                        pe.wait_ge(y_ready, n(e) - 2)
                    for f in range(KB):
                        last = nc.tensor.matmul(l2_bank[e % 2][:, :], h1T[:, e % 2, f, :], w2_sb[:, e % WBUF, f, :],
                                                start=(f == 0), stop=(f == KB - 1))
                    last.then_inc(l2_done, 1)

                turn(0)
                for e in range(NE):
                    if e + 1 < NE:
                        turn(e + 1)
                    layer1(e)
                    if e >= 1:
                        layer2(e - 1)
                layer2(NE - 1)

            pe.wait_ge(over_flag, 1)
            round_pe(0)
            more = pe.value_load(flags[0:1, 1:2])
            with pe.If(more != 0):
                with pe.Fori(1, ROUNDS) as r:
                    round_pe(r)


_INS = ['x', 'src', 'dst', 'L0_gnn_W', 'L0_gnn_b_w', 'L0_gnn_a', 'L0_gnn_b_a', 'L0_ffn_Wr', 'L0_ffn_br', 'L0_ffn_W1',
        'L0_ffn_b1', 'L0_ffn_W2', 'L0_ffn_b2']


def kernel(**inputs):
    import numpy as _np
    import concourse.bacc as _bacc
    from concourse import mybir as _mybir
    from concourse.bass_utils import run_bass_kernel_spmd as _run

    nc = _bacc.Bacc("TRN2", target_bir_lowering=False, num_devices=1)
    arrays, args = {}, []
    for name in _INS:
        a = _np.ascontiguousarray(inputs[name])
        if a.ndim == 0:
            a = a.reshape(1)
        arrays[f"in_{name}_dram"] = a
        args.append(nc.dram_tensor(f"in_{name}_dram", a.shape, _mybir.dt.from_np(a.dtype), kind="ExternalInput").ap())
    args.append(nc.dram_tensor("out_0_dram", (N, D), _mybir.dt.float32, kind="ExternalOutput").ap())
    gnn_ffn(nc, *args)
    r = _run(nc, [arrays], core_ids=[0])
    return r.results[0]["out_0_dram"]
```

```python
from contextlib import ExitStack

import concourse.bass as bass
from concourse import mybir

F32 = mybir.dt.float32
BF16 = mybir.dt.bfloat16
F32R = mybir.dt.float32r
I32 = mybir.dt.int32
U32 = mybir.dt.uint32
ALU = mybir.AluOpType
ACT = mybir.ActivationFunctionType
AX_X = mybir.AxisListType.X

N = 625
D = 512
E = 20000
NE = 8
NB = 5
BP = N // NB
KB = D // 128
EPS = 1e-5
SLOPE = 0.2
MAX_W = 3e38
MIN_DEN = 1e-38

CH = 128
NCH = -(-E // CH)
TAIL = E - (NCH - 1) * CH
HC = (NCH - 1) // 2
STEP = N * CH // E
WIN = 24
BEFORE = 10
GN = 100
NG = -(-N // GN)
NP = NG * GN
GW = GN * NB
WC = WIN * NB
BAT = 5
NBAT = -(-NCH // BAT)
LATE_H = (24, 46)
EARLY_AGG = (114,) * NB
BUSY_START = 15
BUSY_GAP = 3
SMALL_AFTER = 12
WEIGH = {q: g for g, q in enumerate((22, 23, 25, 27, 29))}
RB = 16
RING = RB * BAT
OHW = CH + WC

CAP = 128
ROUNDS = -(-N // CAP)
ROW = D + 5
GATE, TOK, MEAN, VAR, RSTD = D, D + 1, D + 2, D + 3, D + 4
HH = D // 2 + 1
FAR = 65536.0
BASE = 4096.0
NO_TOKEN = 1 << 20
SPLIT_FROM = 1
WBUF = 4


IDENTITY, BANDS, ONES_COLUMN, ONES_B, PADDING, ORDER = range(1, 7)


def gnn_ffn(nc, x, src, dst, w_gnn, b_w, a, b_a, w_r, b_r, w1, b1, w2, b2, out):
    ctx = ExitStack()
    with ctx:
        offset = {}

        def sb(name, shape, dt=F32):
            offset[name] = -(-nc.sbuf_base // 32) * 32
            return ctx.enter_context(nc.sbuf_tensor(name, shape, dt))

        def over(host, skip, name, shape):
            return nc.alloc_sbuf_tensor_at(name, shape, F32R, offset=offset[host] + 4 * skip)

        def sem(name):
            return ctx.enter_context(nc.semaphore(name))

        rows = sb("rows", [BP, NB, ROW])
        xn = sb("xn", [BP, NB, D])
        xnT = sb("xnT", [128, KB, N])
        hx = sb("hx", [BP, NB, D + 3])
        wexp_xsT = sb("wexp_xsT", [128, NB * NP])
        wexp = wexp_xsT[0:BP, :].rearrange("p (k n) -> p k n", k=NB)
        wt_fill = sb("wt_fill", [128, NB * NP])
        fill = wt_fill[:, 0:ROW]
        wt = wt_fill[0:BP, :].rearrange("p (k n) -> p k n", k=NB)
        diag_place0 = sb("diag_place0", [BP, NB * CAP])
        diag = diag_place0[:, 0:N].rearrange("p (k n) -> p k n", k=NB)
        place0 = diag_place0[:, :].rearrange("p (b n) -> p b n", b=NB)
        sd_low = sb("sd_low", [BP, N])
        wg = sb("wg", [128, KB, D + 2])
        a_bc = sb("a_bc", [128, 2, D])
        bw_bc = sb("bw_bc", [128, D])
        c_src = sb("c_src", [128, 2])
        ba_bc = sb("ba_bc", [128, 1])
        wr_sb = sb("wr_sb", [128, KB, NE])
        br_bc = sb("br_bc", [BP, NE])
        b1_row = sb("b1_row", [NE * KB, 128])
        b1T = sb("b1T", [128, NE * KB])
        w1_sb = sb("w1_sb", [128, WBUF, KB, D])
        w2_sb = sb("w2_sb", [128, WBUF, KB, D])
        ring_xs = sb("ring_xs", [128, RING * OHW // 2])
        ring = ring_xs[:, :].bitcast(BF16).rearrange("p (s w) -> p s w", s=RING)
        xs = ring_xs[:, 0:NE * ROW].rearrange("p (e r) -> p e r", e=NE)
        b2_bc = ring_xs[:, NE * ROW:NE * (ROW + D)].rearrange("p (e n) -> p e n", e=NE)
        xs_n, xsT, h1T = (wexp_xsT[:, i * 2 * D:(i + 1) * 2 * D] for i in range(3))
        xs_n = xs_n.rearrange("p (s n) -> p s n", s=2)
        xsT = xsT.rearrange("p (s k n) -> p s k n", s=2, k=KB)
        h1T = h1T.rearrange("p (s k n) -> p s k n", s=2, k=KB)

        w2_hi = [over("wt_fill", 0, "w2_hi0", [128, KB, D]), over("xnT", 0, "w2_hi1", [128, KB, D])]
        h1_hi = over("wt_fill", KB * D, "h1_hi", [128, 2, KB, CAP])
        w2_lo = over("w2_sb", 0, "w2_lo", [128, WBUF, KB, D])
        h1_lo = over("wexp_xsT", 4 * D, "h1_lo", [128, 2, KB, CAP])

        edge_i = sb("edge_i", [128, 2, 2, CH], I32)
        edge_f = sb("edge_f", [128, 2, 2, CH])
        key_f = sb("key_f", [128, 2, 2, CH])
        hi_f = sb("hi_f", [128, 2, CH])
        keyT = sb("keyT", [128, 2, NCH])
        keyrel = sb("keyrel", [128, NCH])
        key_d = sb("key_d", [128, 2, NCH, 2], BF16)
        clipped = sb("clipped", [128, NCH])
        shift = sb("shift", [128, NCH])
        iota_b = sb("iota_b", [128, CH], BF16)
        iota_g = sb("iota_g", [128, GW])
        gen_ab = edge_f[:, 0, :, :].rearrange("p s c -> p (s c)").bitcast(BF16)
        gen_a = edge_f[:, 1, 0, :].bitcast(BF16)[:, 0:CH]
        gen_b = gen_ab[:, 0:GW]
        ones_f = sb("ones_f", [128, 128])
        ones_b = sb("ones_b", [128, 128], BF16)
        zeros_b = sb("zeros_b", [128, 512], BF16)
        ident = sb("ident", [128, 128])
        lower = sb("lower", [BP, BP], BF16)
        bad = sb("bad", [128, 1])
        flags = sb("flags", [1, 2], I32)
        stats = sb("stats", [BP, 2, 6])
        mv = sb("mv", [BP, NB, 2])
        rstd1 = sb("rstd1", [BP, NB])
        vare = sb("vare", [BP, NB])
        minus_half = sb("minus_half", [BP, 1])
        junk = wexp_xsT[:, 0:(KB - 1) * 2 * D].rearrange("p (t n) -> p t n", n=D)
        junk_p = wt_fill[:, ROW:ROW + 3 * D].rearrange("p (t n) -> p t n", t=3)
        shift1 = sb("shift1", [BP, NB])
        warm = sb("warm", [BP, 1])
        s_low = sb("s_low", [BP, NB])
        s_rest = sb("s_rest", [BP, NB])
        minus_wr = sb("minus_wr", [BP, NE])
        den = sb("den", [BP, 2, 2])
        first_slot = sb("first_slot", [BP, NE])
        raw = sb("raw", [BP, NB, NE])
        lg = sb("lg", [BP, NB, NE])
        mx = sb("mx", [BP, NB])
        cand = sb("cand", [BP, NB, NE])
        emin = sb("emin", [BP, NB])
        hot = sb("hot", [BP, NB, NE], BF16)
        shifted = sb("shifted", [BP, NB, NE])
        gate_e = sb("gate_e", [BP, NB, NE])
        gsum = sb("gsum", [BP, NB])
        prod = sb("prod", [BP, NB, NE])
        rank = sb("rank", [BP, NB])
        over = sb("over", [BP, NB])
        under = sb("under", [BP, NB])
        slot_i = sb("slot_i", [BP, NB], I32)
        novr = sb("novr", [BP, 1])
        xs_dram = nc.dram_tensor("xs_dram", [NE * CAP, ROW], F32, kind="Internal").ap()

        pb = [ctx.enter_context(nc.psum_tensor(f"pb{i}", [128, 512], F32)) for i in range(8)]
        turn_bank = [pb[6], pb[7]]
        key_bank = pb[5]
        bad_sum = pb[4][0:1, 40:41]
        b1_ps = pb[4][:, 0:NE * KB]
        wr_ps = pb[4][0:BP, 64:64 + NE]
        h_bank = [pb[1], pb[2], pb[3]]
        sdst_bank = pb[6]
        sdst_last = pb[7][:, 0:BP]
        count_bank = [pb[4], pb[5], pb[0], pb[1], pb[2], pb[3], pb[4]]
        gen_bank = pb[4]
        agg_bank = [(pb[6], pb[7]), (pb[5], pb[0])]
        turn2_bank = pb[1]
        logit_bank, rank_bank = pb[3], pb[4]
        over_sum = pb[3][0:1, 64:65]
        xsT_bank = [pb[2], pb[1]]
        l1_bank = [(pb[3], pb[4]), (pb[5], pb[6])]
        l2_bank = [pb[7], pb[0]]

        x_loaded = [sem(f"x_loaded{b}") for b in range(NB)]
        edges_loaded = sem("edges_loaded")
        edges_padded = sem("edges_padded")
        wg_loaded = [sem(f"wg_loaded{k}") for k in range(2)]
        a_loaded = sem("a_loaded")
        ba_loaded = sem("ba_loaded")
        bw_loaded = sem("bw_loaded")
        small_loaded = sem("small_loaded")
        b2_loaded = sem("b2_loaded")
        w_loaded = [sem(f"w_loaded{e}") for e in range(NE)]
        fill_made = sem("fill_made")
        fill_stored = sem("fill_stored")
        pool_chain = sem("pool_chain")
        ones_made = sem("ones_made")
        consts_made = sem("consts_made")
        dve_chain = sem("dve_chain")
        keys_made = sem("keys_made")
        keys_turned = sem("keys_turned")
        keys_copied = sem("keys_copied")
        bad_made = sem("bad_made")
        bad_flag = sem("bad_flag")
        xn_ready = sem("xn_ready")
        var_ready = sem("var_ready")
        rstd_ready = sem("rstd_ready")
        xn_turned = sem("xn_turned")
        xnT_ready = sem("xnT_ready")
        sdst_done = sem("sdst_done")
        diag_ready = sem("diag_ready")
        s_low_ready = sem("s_low_ready")
        c_summed = sem("c_summed")
        relu_z = sem("relu_z")
        leaky_even = sem("leaky_even")
        leaky_odd = sem("leaky_odd")
        h_biased = sem("h_biased")
        sd_low_ready = sem("sd_low_ready")
        wa_pool = sem("wa_pool")
        wa_ready = sem("wa_ready")
        minus_wr_ready = sem("minus_wr_ready")
        small_summed = sem("small_summed")
        x2_ready = sem("x2_ready")
        shift_ready = sem("shift_ready")
        logits_done = sem("logits_done")
        hot_ready = sem("hot_ready")
        ranks_done = sem("ranks_done")
        gates_exp = sem("gates_exp")
        wexp_ready = sem("wexp_ready")
        h_done = sem("h_done")
        h_copied = sem("h_copied")
        onehots_made = sem("onehots_made")
        onehots_free = sem("onehots_free")
        counts_done = sem("counts_done")
        wt_done = sem("wt_done")
        gen_made = sem("gen_made")
        gen_used = sem("gen_used")
        gen_counted = sem("gen_counted")
        gen_wt = sem("gen_wt")
        first_redone = sem("first_redone")
        agg_done = sem("agg_done")
        xn2_ready = sem("xn2_ready")
        placed = sem("placed")
        xn2_turned = sem("xn2_turned")
        xn2T_ready = sem("xn2T_ready")
        b1T_ready = sem("b1T_ready")
        over_made = sem("over_made")
        over_summed = sem("over_summed")
        over_flag = sem("over_flag")
        slots_ready = sem("slots_ready")
        rows_scattered = sem("rows_scattered")
        xs_loaded = [sem(f"xs_loaded{e}") for e in range(NE)]
        xs_n_ready = sem("xs_n_ready")
        xs_turned = sem("xs_turned")
        xsT_ready = sem("xsT_ready")
        l1_half = sem("l1_half")
        pool_gate = sem("pool_gate")
        l1_done = sem("l1_done")
        relu_act = sem("relu_act")
        relu_dve = sem("relu_dve")
        w2_hi_made = sem("w2_hi_made")
        w2_split = sem("w2_split")
        h1_split = sem("h1_split")
        l2_done = sem("l2_done")
        b2_sum = sem("b2_sum")
        round_chain = sem("round_chain")
        slot_chain = sem("slot_chain")
        y_ready = sem("y_ready")
        out_written = sem("out_written")

        block = ctx.enter_context(nc.Block())

        def rows_of(t, b, w=D):
            return t[b * BP:(b + 1) * BP, 0:w]

        SPLIT = range(SPLIT_FROM, NE)

        HALVES = [(0, 0), (1, 0)] + [(b, 1) for b in range(NB)] + [(b, 0) for b in range(2, NB)]

        def copies(b, t):
            return HALVES.index((b, t)) + 1

        @block.sync
        def _(sp):
            for b in range(NB):
                sp.dma_start(rows[:, b, 0:D], rows_of(x, b)).then_inc(x_loaded[b], 16)
            sp.dma_start(a_bc[:, :, :], a.rearrange("(t n) -> t n", t=2).partition_broadcast(128)).then_inc(a_loaded, 16)
            for k in range(2):
                sp.dma_start(wg[:, 2 * k:2 * k + 2, 0:D],
                             w_gnn[k * 256:(k + 1) * 256, :].rearrange("(k p) n -> p k n", p=128)).then_inc(wg_loaded[k], 16)
            sp.dma_start(bw_bc[:, :], b_w.partition_broadcast(128)).then_inc(bw_loaded, 16)
            sp.dma_start(ba_bc[:, :], b_a.partition_broadcast(128)).then_inc(ba_loaded, 16)
            sp.dma_start(wr_sb[:, :, :], w_r.rearrange("(k p) n -> p k n", p=128)).then_inc(small_loaded, 16)
            sp.dma_start(br_bc[:, :], b_r.partition_broadcast(BP)).then_inc(small_loaded, 16)
            sp.dma_start(b1_row[:, :], b1.rearrange("e (k p) -> (e k) p", p=128)).then_inc(small_loaded, 16)
            sp.wait_ge(fill_made, 1)
            sp.dma_start(xs_dram.rearrange("(e p) r -> p e r", p=CAP),
                         fill[:, :].unsqueeze(1).to_broadcast([128, NE, ROW])).then_inc(fill_stored, 16)

            def load_weights(r, e):
                n = r * NE + e
                if not (isinstance(n, int) and n < WBUF):
                    sp.wait_ge(l2_done, n - WBUF + 1)
                sp.dma_start(w1_sb[:, e % WBUF, :, :],
                             w1[e].rearrange("(k p) f -> p k f", p=128)).then_inc(w_loaded[e], 16)
                sp.dma_start(w2_sb[:, e % WBUF, :, :],
                             w2[e].rearrange("(k p) f -> p k f", p=128)).then_inc(w_loaded[e], 16)

            def load_slots(r):
                sp.wait_ge(rows_scattered, (r + 1) * (16 * NB))
                for e in (1, 0, *range(2, NE)):
                    sp.dma_start(xs[:, e, :], xs_dram[e * CAP:(e + 1) * CAP, :]).then_inc(xs_loaded[e], 16)

            for e in range(WBUF):
                load_weights(0, e)
            sp.wait_ge(wt_done, NG)
            sp.dma_start(b2_bc, b2.partition_broadcast(128)).then_inc(b2_loaded, 16)
            load_slots(0)
            for e in range(WBUF, NE):
                load_weights(0, e)

            sp.wait_ge(over_flag, 1)
            more = sp.value_load(flags[0:1, 1:2])
            with sp.If(more != 0):
                with sp.Fori(1, ROUNDS) as r:
                    for e in range(WBUF):
                        load_weights(r, e)
                    sp.wait_ge(out_written, r * (16 * NE))
                    load_slots(r)
                    for e in range(WBUF, NE):
                        load_weights(r, e)

        @block.gpsimd
        def _(pool):
            chain = [0]

            def link(ins):
                chain[0] += 1
                ins.then_inc(pool_chain, 1)
                pool.wait_ge(pool_chain, chain[0])

            nc.gpsimd.memset(edge_i[:, 0, :, :], -1).then_inc(edges_padded, 1)
            nc.gpsimd.memset(edge_i[:, 1, :, :], N - 1).then_inc(edges_padded, 1)
            nc.gpsimd.memset(ones_f[:, :], 1.0).then_inc(ones_made, 1)
            link(nc.gpsimd.memset(ident[:, :], 0.0))
            nc.gpsimd.affine_select(out=ident[:, :], in_=ident[:, :], compare_op=ALU.not_equal, fill=1.0,
                                    base=0, pattern=[[-1, 128]], channel_multiplier=1).then_inc(consts_made, 1)
            nc.gpsimd.iota(iota_b[:, :], pattern=[[1, CH]], base=0, channel_multiplier=0,
                           allow_small_or_imprecise_dtypes=True)
            nc.gpsimd.iota(shift[:, :], pattern=[[STEP * NB, NCH]], base=-BEFORE * NB, channel_multiplier=0,
                           allow_small_or_imprecise_dtypes=True).then_inc(consts_made, 1)
            link(nc.gpsimd.memset(minus_half[:, :], -0.5))
            link(nc.gpsimd.memset(fill[:, :], 0.0))
            nc.gpsimd.memset(fill[:, TOK:TOK + 1].bitcast(I32), NO_TOKEN).then_inc(fill_made, 1)

            for b0, b1 in ((0, 1), (1, 3), (3, 5)):
                pool.wait_ge(var_ready, b1)
                nb = b1 - b0
                nc.gpsimd.tensor_scalar(shift1[:, b0:b1], mv[:, b0:b1, 0], -1.0, None, ALU.mult)
                link(nc.gpsimd.tensor_scalar(vare[:, b0:b1], mv[:, b0:b1, 1], EPS, None, ALU.add))
                link(nc.gpsimd.tensor_tensor(rstd1[:, b0:b1], vare[:, b0:b1], minus_half[:, :].to_broadcast([BP, nb]),
                                             ALU.pow))
                nc.gpsimd.tensor_tensor(shift1[:, b0:b1], shift1[:, b0:b1], rstd1[:, b0:b1],
                                        ALU.mult).then_inc(rstd_ready, nb)
            pool.wait_ge(a_loaded, 16)
            pool.wait_ge(wg_loaded[1], 16)
            for t in range(2):
                nc.gpsimd.tensor_tensor(junk_p[:, t, :], wg[:, KB - 1, 0:D], a_bc[:, t, :], ALU.mult).then_inc(wa_pool, 1)
            link(nc.gpsimd.tensor_tensor(junk_p[:, 2, :], a_bc[:, 0, :], a_bc[:, 1, :], ALU.add))
            pool.wait_ge(bw_loaded, 16)
            nc.gpsimd.tensor_tensor(junk_p[:, 2, :], junk_p[:, 2, :], bw_bc[:, :], ALU.mult).then_inc(wa_pool, 1)
            nc.gpsimd.memset(hx[:, :, D + 2:D + 3], 1.0).then_inc(consts_made, 1)
            pool.wait_ge(ba_loaded, 16)
            pool.wait_ge(c_summed, 1)
            link(nc.gpsimd.tensor_tensor(c_src[:, 1:2], c_src[:, 0:1], ba_bc[:, :], ALU.add))

            def add_bias(k, t):
                at = slice(0, HH) if t == 0 else slice(HH, D)
                pool.wait_ge(h_copied, copies(k, t))
                nc.gpsimd.tensor_tensor(hx[:, k, at], hx[:, k, at], bw_bc[0:BP, at], ALU.add).then_inc(h_biased, 1)

            for k in range(NB):
                pool.wait_ge(h_copied, copies(k, 1))
                link(nc.gpsimd.tensor_tensor(hx[:, k, D + 1:D + 2], hx[:, k, D + 1:D + 2], c_src[0:BP, 1:2], ALU.add))
                nc.gpsimd.tensor_scalar(s_low[:, k:k + 1], hx[:, k, D + 1:D + 2], SLOPE, None, ALU.mult)
                nc.gpsimd.tensor_scalar(s_rest[:, k:k + 1], hx[:, k, D + 1:D + 2], 1.0 - SLOPE, None,
                                        ALU.mult).then_inc(s_low_ready, 1)
                add_bias(k, 1)
            nc.gpsimd.memset(zeros_b[:, :], 0.0)
            nc.gpsimd.memset(ones_b[:, :], 1.0).then_inc(consts_made, 1)
            nc.gpsimd.memset(wexp[:, :, N:NP], 0.0).then_inc(consts_made, 1)
            for k in range(0, NB, 2):
                pool.wait_ge(relu_z, k + 1)
                pool.wait_ge(sd_low_ready, 1)
                nc.gpsimd.tensor_tensor(wexp[:, k, 0:N], wexp[:, k, 0:N], sd_low[:, :], ALU.add).then_inc(leaky_even, 1)
            for k in range(NB):
                add_bias(k, 0)
            nc.gpsimd.iota(rows[:, :, TOK:TOK + 1].bitcast(I32), pattern=[[BP, NB], [0, 1]], base=0, channel_multiplier=1)
            nc.gpsimd.iota(first_slot[:, :], pattern=[[CAP, NE]], base=-int(BASE), channel_multiplier=0,
                           allow_small_or_imprecise_dtypes=True)
            nc.gpsimd.iota(iota_g[:, :], pattern=[[1, GW]], base=0, channel_multiplier=0,
                           allow_small_or_imprecise_dtypes=True)
            link(nc.gpsimd.memset(lower[:, :], 1.0))
            nc.gpsimd.affine_select(out=lower[:, :], in_=lower[:, :], compare_op=ALU.is_gt, fill=0.0,
                                    base=0, pattern=[[1, BP]], channel_multiplier=-1).then_inc(consts_made, 1)

            def inv_std(b):
                pool.wait_ge(var_ready, NB + b + 1)
                link(nc.gpsimd.tensor_scalar(vare[:, b:b + 1], rows[:, b, VAR:VAR + 1], EPS, None, ALU.add))
                nc.gpsimd.tensor_tensor(rows[:, b, RSTD:RSTD + 1], vare[:, b:b + 1], minus_half[:, :],
                                        ALU.pow).then_inc(rstd_ready, 1)

            slot_bound = pool.to_reg(NE * CAP - 1)
            token_bound = pool.to_reg(N - 1)

            def scatter_rows(r, b):
                pool.wait_ge(slots_ready, r * NB + b + 1)
                pool.sem_inc(pool_gate, 1)
                pool.indirect_dma_start(
                    out=xs_dram, out_offset=bass.IndirectOffsetOnAxis(ap=slot_i[:, b:b + 1].bitcast(U32), axis=0),
                    in_=rows[:, b, :], in_offset=None, bounds_check=slot_bound,
                    oob_is_err=False).then_inc(rows_scattered, 16)

            def scatter_out(r):
                for e in range(NE):
                    pool.wait_ge(y_ready, r * NE + e + 1)
                    pool.sem_inc(pool_gate, 1)
                    pool.indirect_dma_start(
                        out=out, out_offset=bass.IndirectOffsetOnAxis(ap=xs[:, e, TOK:TOK + 1].bitcast(U32), axis=0),
                        in_=xs[:, e, 0:D], in_offset=None, bounds_check=token_bound,
                        oob_is_err=False).then_inc(out_written, 16)

            pool.wait_ge(fill_stored, 16)
            inv_std(0)
            for b in range(NB):
                if b + 1 < NB:
                    inv_std(b + 1)
                scatter_rows(0, b)
            scatter_out(0)
            pool.wait_ge(out_written, 16 * NE)
            pool.wait_ge(over_flag, 1)
            more = pool.value_load(flags[0:1, 1:2])
            with pool.If(more != 0):
                with pool.Fori(1, ROUNDS) as r:
                    for b in range(NB):
                        scatter_rows(r, b)
                    scatter_out(r)
                    pool.wait_ge(out_written, r * (16 * NE) + 16 * NE)
                nc.gpsimd.engine_nop()

        @block.scalar
        def _(act):
            act.wait_ge(ones_made, 1)
            nc.scalar.activation(warm[:, :], ones_f[0:BP, 0:1], ACT.Exp)
            act.wait_ge(edges_padded, 2)
            for s, t in enumerate((src, dst)):
                act.dma_start(edge_i[0:HC, s, :, :],
                              t[0:2 * HC * CH].rearrange("(h p c) -> p h c", p=HC, c=CH)).then_inc(edges_loaded, 16)
                act.dma_start(edge_i[HC:HC + 1, s, 1, 0:TAIL], t[2 * HC * CH:E].unsqueeze(0)).then_inc(edges_loaded, 16)

            def normalise_block(b):
                act.wait_ge(rstd_ready, b + 1)
                nc.scalar.activation(xn[:, b, :], rows[:, b, 0:D], ACT.Identity, bias=shift1[:, b:b + 1],
                                     scale=rstd1[:, b:b + 1]).then_inc(xn_ready, 1)

            def copy_xnT(b):
                act.wait_ge(xn_turned, b + 1)
                nc.scalar.copy(xnT[:, :, b * BP:(b + 1) * BP],
                               turn_bank[b % 2][:, 0:KB * BP].rearrange("p (k n) -> p k n", k=KB)).then_inc(xnT_ready, 1)

            normalise_block(0)
            for b in range(NB):
                if b + 1 < NB:
                    normalise_block(b + 1)
                copy_xnT(b)
            act.wait_ge(keys_turned, 1)
            nc.scalar.copy(keyT[:, :, :], key_bank[:, 0:2 * NCH].rearrange("p (s c) -> p s c", s=2)).then_inc(keys_copied, 1)

            def sum_products(t, to):
                act.wait_ge(wa_pool, t + 1)
                return nc.scalar.activation(junk_p[:, t, :], junk_p[:, t, :], ACT.Copy, accum_out=to)

            def copy_h(i):
                b, t = HALVES[i]
                act.wait_ge(h_done, i + 1)
                at = slice(t * HH, (t + 1) * HH)
                nc.scalar.copy(hx[:, b, at], h_bank[i % 3][0:BP, 0:HH]).then_inc(h_copied, 1)

            def relu_08z(k):
                act.wait_ge(s_low_ready, k + 1)
                nc.scalar.activation(wexp[:, k, 0:N], sd_low[:, :], ACT.Relu, bias=s_rest[:, k:k + 1],
                                     scale=(1.0 - SLOPE) / SLOPE).then_inc(relu_z, 1)

            def exp_leaky(k):
                act.wait_ge(leaky_odd if k % 2 else leaky_even, k // 2 + 1)
                nc.scalar.activation(wexp[:, k, 0:N], wexp[:, k, 0:N], ACT.Exp, bias=s_low[:, k:k + 1]).then_inc(wexp_ready, 1)

            copy_h(0)
            for t in range(2):
                sum_products(t, wg[:, KB - 1, D + t:D + t + 1]).then_inc(wa_ready, 1)
            copy_h(1)
            sum_products(2, c_src[:, 0:1]).then_inc(c_summed, 1)
            act.wait_ge(consts_made, IDENTITY)
            for k in range(NB):
                copy_h(2 + k)
                act.wait_ge(h_copied, 3 + k)
                nc.scalar.activation(diag[:, k, :], ident[0:BP, 0:BP], ACT.Copy,
                                     scale=hx[:, k, D:D + 1]).then_inc(diag_ready, 1)
            act.wait_ge(sdst_done, 1)
            nc.scalar.activation(sd_low[:, 0:4 * BP], sdst_bank[0:BP, 0:4 * BP], ACT.Copy, scale=SLOPE)
            nc.scalar.activation(sd_low[:, 4 * BP:N], sdst_last[0:BP, :], ACT.Copy, scale=SLOPE).then_inc(sd_low_ready, 1)
            act.wait_ge(sd_low_ready, 1)
            relu_08z(0)
            relu_08z(1)
            copy_h(7)
            relu_08z(2)
            exp_leaky(1)
            relu_08z(3)
            copy_h(8)
            exp_leaky(0)
            relu_08z(4)
            exp_leaky(3)
            exp_leaky(2)
            exp_leaky(4)
            copy_h(9)

            def copy_x2T(b):
                act.wait_ge(xn2_turned, b + 1)
                nc.scalar.copy(xnT[:, :, b * BP:(b + 1) * BP],
                               turn2_bank[:, 0:KB * BP].rearrange("p (k n) -> p k n", k=KB)).then_inc(xn2T_ready, 1)

            def gate(b):
                act.wait_ge(shift_ready, b + 1)
                nc.scalar.activation(gate_e[:, b, :], shifted[:, b, :], ACT.Exp,
                                     accum_out=gsum[:, b:b + 1]).then_inc(gates_exp, 1)

            for b in range(NB):
                copy_x2T(b)
                gate(b)

            def round_act(r):
                static = isinstance(r, int)

                def copy_xsT(e):
                    act.wait_ge(xs_turned, r * NE + e + 1)
                    if not (static and e < 2):
                        act.wait_ge(l1_done, r * NE + e - 1)
                    nc.scalar.copy(xsT[:, e % 2, :, :],
                                   xsT_bank[e % 2][:, :].rearrange("p (k n) -> p k n", k=KB)).then_inc(xsT_ready, 1)

                copy_xsT(0)
                for e in range(NE):
                    relu(r, e)
                    if e + 1 < NE and not (static and e == 1):
                        copy_xsT(e + 1)
                    if static and e == 0:
                        copy_xsT(2)
                    if static and e + 1 in SPLIT:
                        act.wait_ge(w_loaded[e + 1], 32)
                        if e + 1 < SPLIT_FROM + 2:
                            act.wait_ge(agg_done, NB)
                            act.wait_ge(logits_done, NB)
                        else:
                            act.wait_ge(l2_done, e)
                        nc.scalar.copy(w2_hi[(e + 1) % 2][:, :, :], w2_sb[:, (e + 1) % WBUF, :, :]).then_inc(w2_hi_made, 1)

            def relu(r, e):
                act.wait_ge(l1_half, r * NE + e + 1)
                if not (isinstance(r, int) and e < 2):
                    act.wait_ge(l2_done, r * NE + e - 1)
                for f in range(2):
                    last = nc.scalar.activation(h1T[:, e % 2, f, :], l1_bank[e % 2][0][:, f * CAP:(f + 1) * CAP], ACT.Relu,
                                                bias=b1T[:, e * KB + f:e * KB + f + 1])
                    if isinstance(r, int) and e in SPLIT:
                        last = nc.scalar.activation(h1_hi[:, e % 2, f, :], l1_bank[e % 2][0][:, f * CAP:(f + 1) * CAP],
                                                    ACT.Relu, bias=b1T[:, e * KB + f:e * KB + f + 1])
                last.then_inc(relu_act, 1)

            round_act(0)
            act.wait_ge(over_flag, 1)
            more = act.value_load(flags[0:1, 1:2])
            with act.If(more != 0):
                with act.Fori(1, ROUNDS) as r:
                    round_act(r)

        @block.vector
        def _(dve):
            chain = [0]

            def link(ins):
                chain[0] += 1
                ins.then_inc(dve_chain, 1)
                dve.wait_ge(dve_chain, chain[0])

            def make_keys():
                live = slice(0, HC + 1)
                dve.wait_ge(edges_loaded, 4 * 16)
                link(nc.vector.tensor_copy(edge_f[live, :, :, :], edge_i[live, :, :, :]))
                srcf, dstf, hi = edge_f[live, 0, :, :], edge_f[live, 1, :, :], hi_f[live, :, :]
                link(nc.vector.tensor_scalar(hi, srcf, float(BP), None, ALU.is_ge))
                for k in range(2, NB):
                    link(nc.vector.scalar_tensor_tensor(hi, srcf, float(BP * k), hi, ALU.is_ge, ALU.add))
                nc.vector.scalar_tensor_tensor(key_f[live, 0, :, :], hi, -float(BP), srcf, ALU.mult, ALU.add)
                nc.vector.scalar_tensor_tensor(key_f[live, 1, :, :], dstf, float(NB), hi, ALU.mult,
                                               ALU.add).then_inc(keys_made, 1)

            for b in range(NB):
                dve.wait_ge(x_loaded[b], 16)
                link(nc.vector.bn_stats(stats[:, b % 2, :], rows[:, b, 0:D]))
                nc.vector.bn_aggr(mv[:, b, :], stats[:, b % 2, :]).then_inc(var_ready, 1)
            make_keys()
            dve.wait_ge(a_loaded, 16)
            for k in range(KB - 1):
                dve.wait_ge(wg_loaded[k // 2], 16)
                for t in range(2):
                    ins = nc.vector.tensor_tensor_reduce(out=junk[:, 2 * k + t, :], in0=wg[:, k, 0:D], in1=a_bc[:, t, :],
                                                         scale=1.0, scalar=0.0, op0=ALU.mult, op1=ALU.add,
                                                         accum_out=wg[:, k, D + t:D + t + 1])
            ins.then_inc(wa_ready, 1)
            dve.wait_ge(keys_copied, 1)
            dve.wait_ge(consts_made, BANDS)
            link(nc.vector.tensor_tensor(keyrel[:, :], keyT[:, 1, :], shift[:, :], ALU.subtract))
            for s, t in enumerate((keyT[:, 0, :], keyrel[:, :])):
                ins = nc.vector.tensor_copy(key_d[:, s, :, :], t.unsqueeze(2).to_broadcast([128, NCH, 2]))
            link(ins)

            def onehots(q):
                n = min(BAT, NCH - q * BAT)
                if q >= RB:
                    dve.wait_ge(onehots_free, q - RB + 1)
                to = ring[:, (q % RB) * BAT:(q % RB) * BAT + n, :]
                for s, c0, w in ((0, 0, CH), (1, CH, WC)):
                    shape = [128, n, w // 2, 2]
                    ins = nc.vector.tensor_tensor(
                        to[:, :, c0:c0 + w].rearrange("p c (w t) -> p c w t", t=2),
                        iota_b[:, 0:w].rearrange("p (w t) -> p w t", t=2).unsqueeze(1).to_broadcast(shape),
                        key_d[:, s, q * BAT:q * BAT + n, :].unsqueeze(2).to_broadcast(shape), ALU.is_equal)
                ins.then_inc(onehots_made, 1)

            def weigh(g, ready, ps, done):
                at = bass.ds(g * GN, GN)
                dve.wait_ge(*ready)
                nc.vector.scalar_tensor_tensor(wt[:, :, at], wexp[:, :, at], MAX_W,
                                               ps[0:BP, 0:GW].rearrange("p (n k) -> p k n", k=NB),
                                               ALU.min, ALU.mult).then_inc(done, 1)

            def weigh_band(g):
                weigh(g, (counts_done, g + 1), count_bank[g], wt_done)

            for q in range(RB):
                onehots(q)
                if q == SMALL_AFTER:
                    dve.wait_ge(small_summed, 1)
                    nc.vector.tensor_copy(flags[0:1, 0:1], bad_sum).then_inc(bad_flag, 1)
                    nc.vector.tensor_copy(b1T[:, :], b1_ps).then_inc(b1T_ready, 1)
                    nc.vector.tensor_scalar(minus_wr[:, :], wr_ps, -1.0, None, ALU.mult).then_inc(minus_wr_ready, 1)
                if q == 0:
                    link(nc.vector.tensor_scalar(clipped[:, :], keyrel[:, :], 0.0, float(WC - 1), ALU.max, ALU.min))
                    link(nc.vector.tensor_tensor(clipped[:, :], clipped[:, :], keyrel[:, :], ALU.not_equal))
                    nc.vector.tensor_reduce(bad[:, :], clipped[:, :], AX_X, ALU.add).then_inc(bad_made, 1)
            for q in range(RB, NBAT):
                if q - RB in (0, 1):
                    k = 2 * (q - RB) + 1
                    dve.wait_ge(relu_z, k + 1)
                    dve.wait_ge(sd_low_ready, 1)
                    nc.vector.tensor_tensor(wexp[:, k, 0:N], wexp[:, k, 0:N], sd_low[:, :], ALU.add).then_inc(leaky_odd, 1)
                onehots(q)
                if q in WEIGH:
                    if WEIGH[q] == 0:
                        dve.wait_ge(consts_made, PADDING)
                        dve.wait_ge(fill_stored, 16)
                        dve.wait_ge(wexp_ready, NB)
                    weigh_band(WEIGH[q])
            for g in range(len(WEIGH), NG):
                weigh_band(g)

            dve.wait_ge(bad_flag, 1)
            outside = dve.value_load(flags[0:1, 0:1])
            with dve.If(outside != 0):
                dve.wait_ge(wt_done, NG)
                dve.wait_ge(consts_made, ORDER)
                dve.sem_inc(gen_used, 1)
                dve.sem_inc(gen_wt, 1)
                with dve.Fori(0, NG) as g:
                    with dve.Fori(0, NCH) as c:
                        dve.wait_ge(gen_used, g * NCH + c + 1)
                        nc.vector.tensor_scalar(gen_a[:, :], iota_b[:, :], keyT[:, 0, bass.ds(c, 1)], None, ALU.is_equal)
                        nc.vector.tensor_scalar(gen_b[:, :], iota_g[:, :], keyT[:, 1, bass.ds(c, 1)], None,
                                                ALU.is_equal).then_inc(gen_made, 1)
                    weigh(g, (gen_counted, g + 1), gen_bank, gen_wt)
                    nc.vector.tensor_scalar(keyT[:, 1, :], keyT[:, 1, :], -float(GW), None, ALU.add).then_inc(gen_wt, 1)
                    dve.wait_ge(gen_wt, g * 2 + 3)
                dve.wait_ge(first_redone, NB)

            def add_gnn(b):
                pa, pc = agg_bank[b % 2]
                dve.wait_ge(agg_done, b + 1)
                link(nc.vector.tensor_scalar(den[:, b % 2, 0:1], pc[0:BP, HH:HH + 1], MIN_DEN, None, ALU.max))
                link(nc.vector.reciprocal(den[:, b % 2, 1:2], den[:, b % 2, 0:1]))
                nc.vector.scalar_tensor_tensor(rows[:, b, 0:HH], pa[0:BP, 0:HH], den[:, b % 2, 1:2], rows[:, b, 0:HH],
                                               ALU.mult, ALU.add)
                nc.vector.scalar_tensor_tensor(rows[:, b, HH:D], pc[0:BP, 0:D - HH], den[:, b % 2, 1:2],
                                               rows[:, b, HH:D], ALU.mult, ALU.add).then_inc(x2_ready, 1)
                dve.wait_ge(x2_ready, b + 1)
                link(nc.vector.bn_stats(stats[:, b % 2, :], rows[:, b, 0:D]))
                nc.vector.bn_aggr(rows[:, b, MEAN:MEAN + 2], stats[:, b % 2, :]).then_inc(var_ready, 1)

            def choose(b):
                dve.wait_ge(logits_done, b + 1)
                dve.wait_ge(var_ready, NB + b + 1)
                link(nc.vector.scalar_tensor_tensor(raw[:, b, :], minus_wr[:, :], rows[:, b, MEAN:MEAN + 1],
                                                    logit_bank[0:BP, b * NE:(b + 1) * NE], ALU.mult, ALU.add))
                dve.wait_ge(rstd_ready, NB + b + 1)
                link(nc.vector.scalar_tensor_tensor(lg[:, b, :], raw[:, b, :], rows[:, b, RSTD:RSTD + 1], br_bc[:, :],
                                                    ALU.mult, ALU.add))
                link(nc.vector.tensor_reduce(mx[:, b:b + 1], lg[:, b, :], AX_X, ALU.max))
                link(nc.vector.scalar_tensor_tensor(cand[:, b, :], lg[:, b, :], mx[:, b:b + 1], first_slot[:, :],
                                                    ALU.is_equal, ALU.mult))
                link(nc.vector.tensor_reduce(emin[:, b:b + 1], cand[:, b, :], AX_X, ALU.min))
                nc.vector.tensor_scalar(hot[:, b, :], cand[:, b, :], emin[:, b:b + 1], None,
                                        ALU.is_equal).then_inc(hot_ready, 1)
                nc.vector.tensor_scalar(shifted[:, b, :], lg[:, b, :], mx[:, b:b + 1], None,
                                        ALU.subtract).then_inc(shift_ready, 1)

            def normalise_row(b):
                nc.vector.tensor_scalar(xn[:, b, :], rows[:, b, 0:D], rows[:, b, MEAN:MEAN + 1],
                                        rows[:, b, RSTD:RSTD + 1], ALU.subtract, ALU.mult).then_inc(xn2_ready, 1)

            def place_first(b):
                dve.wait_ge(slots_ready, b + 1)
                nc.vector.tensor_scalar(place0[:, b, :], iota_b[0:BP, 0:CAP], rank[:, b:b + 1], emin[:, b:b + 1],
                                        ALU.subtract, ALU.is_equal).then_inc(placed, 1)

            def find_slot(b):
                dve.wait_ge(gates_exp, b + 1)
                nc.vector.reciprocal(rows[:, b, GATE:GATE + 1], gsum[:, b:b + 1])
                dve.wait_ge(hot_ready, b + 1)
                dve.wait_ge(ranks_done, b + 1)
                link(nc.vector.tensor_tensor_reduce(out=prod[:, b, :], in0=rank_bank[0:BP, b * NE:(b + 1) * NE],
                                                    in1=hot[:, b, :], scale=1.0, scalar=BASE, op0=ALU.mult, op1=ALU.add,
                                                    accum_out=rank[:, b:b + 1]))
                link(nc.vector.tensor_scalar(over[:, b:b + 1], rank[:, b:b + 1], BASE + CAP, FAR, ALU.is_ge, ALU.mult))
                nc.vector.scalar_tensor_tensor(slot_i[:, b:b + 1], rank[:, b:b + 1], emin[:, b:b + 1], over[:, b:b + 1],
                                               ALU.add, ALU.add).then_inc(slots_ready, 1)

            dve.wait_ge(small_loaded, 48)
            dve.wait_ge(consts_made, ORDER)
            dve.wait_ge(minus_wr_ready, 1)
            for b in range(NB):
                add_gnn(b)
                if b >= 1:
                    find_slot(b - 1)
                    place_first(b - 1)
                    normalise_row(b - 1)
                choose(b)
            normalise_row(NB - 1)
            find_slot(NB - 1)
            place_first(NB - 1)
            nc.vector.tensor_reduce(novr[:, :], over[:, :], AX_X, ALU.add).then_inc(over_made, 1)
            dve.wait_ge(over_summed, 1)
            nc.vector.tensor_copy(flags[0:1, 1:2], over_sum).then_inc(over_flag, 1)

            def round_dve(r, step):
                static = isinstance(r, int)

                def n(e):
                    return r * NE + e + 1

                def normalise(e):
                    scale_x(e)
                    add_b2(e)

                def scale_x(e):
                    dve.wait_ge(xs_loaded[e], r * 16 + 16)
                    if not (static and e < 2):
                        dve.wait_ge(xs_turned, n(e) - 2)
                    nc.vector.tensor_scalar(xs_n[:, e % 2, :], xs[:, e, 0:D], xs[:, e, MEAN:MEAN + 1],
                                            xs[:, e, RSTD:RSTD + 1], ALU.subtract, ALU.mult).then_inc(xs_n_ready, 1)

                def add_b2(e):
                    dve.wait_ge(xs_loaded[e], r * 16 + 16)
                    dve.wait_ge(xs_n_ready, n(e))
                    nc.vector.scalar_tensor_tensor(xs[:, e, 0:D], b2_bc[:, e, :], xs[:, e, GATE:GATE + 1],
                                                   xs[:, e, 0:D], ALU.mult, ALU.add).then_inc(step, 1)

                def relu(e):
                    dve.wait_ge(l1_done, n(e))
                    if not (static and e < 2):
                        dve.wait_ge(l2_done, n(e) - 2)
                    for f in range(2, KB):
                        last = nc.vector.tensor_scalar(h1T[:, e % 2, f, :], l1_bank[e % 2][1][:, (f - 2) * CAP:(f - 1) * CAP],
                                                       b1T[:, e * KB + f:e * KB + f + 1], 0.0, ALU.add, ALU.max)
                        if static and e in SPLIT:
                            last = nc.vector.tensor_scalar(h1_hi[:, e % 2, f, :], l1_bank[e % 2][1][:, (f - 2) * CAP:(f - 1) * CAP],
                                                           b1T[:, e * KB + f:e * KB + f + 1], 0.0, ALU.add, ALU.max)
                    last.then_inc(relu_dve, 1)
                    if static and e in SPLIT:
                        dve.wait_ge(relu_act, n(e))
                        dve.wait_ge(relu_dve, n(e))
                        nc.vector.tensor_tensor(h1_lo[:, e % 2, :, :], h1T[:, e % 2, :, :],
                                                h1_hi[:, e % 2, :, :].bitcast(F32), ALU.subtract).then_inc(h1_split, 1)

                def split_w2(e):
                    dve.wait_ge(w2_hi_made, e - SPLIT_FROM + 1)
                    nc.vector.tensor_tensor(w2_lo[:, e % WBUF, :, :], w2_sb[:, e % WBUF, :, :],
                                            w2_hi[e % 2][:, :, :].bitcast(F32), ALU.subtract).then_inc(w2_split, 1)

                def finish(e):
                    dve.wait_ge(l2_done, n(e))
                    dve.wait_ge(step, n(e))
                    nc.vector.scalar_tensor_tensor(xs[:, e, 0:D], l2_bank[e % 2][:, :], xs[:, e, GATE:GATE + 1],
                                                   xs[:, e, 0:D], ALU.mult, ALU.add).then_inc(y_ready, 1)

                if static:
                    dve.sem_inc(xs_n_ready, 1)
                    relu(0)
                    scale_x(1)
                    scale_x(2)
                    for e in range(3):
                        add_b2(e)
                else:
                    normalise(0)
                    normalise(1)
                for e in range(NE):
                    if not (static and e == 0):
                        relu(e)
                    if e + 2 < NE and not (static and e == 0):
                        normalise(e + 2)
                    if e >= 1:
                        finish(e - 1)
                    if static and e + 1 in SPLIT:
                        split_w2(e + 1)
                finish(NE - 1)

            b2_added = b2_sum
            dve.wait_ge(b2_loaded, 16)
            dve.wait_ge(b1T_ready, 1)
            round_dve(0, b2_added)

            dve.wait_ge(over_flag, 1)
            more = dve.value_load(flags[0:1, 1:2])
            with dve.If(more != 0):
                with dve.Fori(1, ROUNDS) as r:
                    dve.wait_ge(rows_scattered, r * (16 * NB))
                    nc.vector.tensor_scalar(rank[:, :], rank[:, :], -float(CAP), None, ALU.add).then_inc(round_chain, 1)
                    dve.wait_ge(round_chain, r * 4 - 3)
                    nc.vector.tensor_scalar(over[:, :], rank[:, :], BASE + CAP, FAR, ALU.is_ge, ALU.mult).then_inc(round_chain, 1)
                    nc.vector.scalar_tensor_tensor(under[:, :], rank[:, :], BASE, emin[:, :], ALU.is_lt,
                                                   ALU.mult).then_inc(round_chain, 1)
                    dve.wait_ge(round_chain, r * 4 - 1)
                    nc.vector.scalar_tensor_tensor(over[:, :], under[:, :], -FAR, over[:, :], ALU.mult,
                                                   ALU.add).then_inc(round_chain, 1)
                    dve.wait_ge(round_chain, r * 4)
                    nc.vector.tensor_tensor(over[:, :], over[:, :], emin[:, :], ALU.add).then_inc(slot_chain, 1)
                    dve.wait_ge(slot_chain, r)
                    nc.vector.tensor_tensor(slot_i[:, :], over[:, :], rank[:, :], ALU.add).then_inc(slots_ready, NB)
                    round_dve(r, b2_added)

        @block.tensor
        def _(pe):
            def keep_busy(n, bank):
                for _ in range(n):
                    nc.tensor.matmul(bank[:, 0:128], ones_f[:, :], ones_f[:, :], start=True, stop=True,
                                     skip_group_check=True)

            pe.wait_ge(ones_made, 1)
            keep_busy(BUSY_START, pb[0])
            pe.wait_ge(consts_made, IDENTITY)
            for b in range(NB):
                pe.wait_ge(xn_ready, b + 1)
                if b >= 2:
                    pe.wait_ge(xnT_ready, b - 1)
                for k in range(KB):
                    last = nc.tensor.transpose(turn_bank[b % 2][:, k * BP:(k + 1) * BP], xn[:, b, k * 128:(k + 1) * 128],
                                               ident[0:BP, 0:BP])
                last.then_inc(xn_turned, 1)
            pe.wait_ge(keys_made, 1)
            for s in range(2):
                for h in range(2):
                    last = nc.tensor.transpose(key_bank[:, s * NCH + h * HC:s * NCH + h * HC + HC + h],
                                               key_f[0:HC + h, s, h, :], ident[0:HC + h, 0:HC + h])
            last.then_inc(keys_turned, 1)

            def project(i):
                b, t = HALVES[i]
                if i >= 3:
                    pe.wait_ge(h_copied, i - 2)
                if i < NB:
                    pe.wait_ge(xnT_ready, b + 1)
                for k in range(KB):
                    if i == 0:
                        pe.wait_ge(wg_loaded[k // 2], 16)
                    if i == 2 and k == 0:
                        pe.wait_ge(wa_ready, 3)
                    last = nc.tensor.matmul(h_bank[i % 3][0:BP, 0:HH], xnT[:, k, b * BP:(b + 1) * BP],
                                            wg[:, k, t * HH:(t + 1) * HH], start=(k == 0), stop=(k == KB - 1))
                last.then_inc(h_done, 1)

            def repeat_sdst():
                for k in range(NB):
                    pe.wait_ge(diag_ready, k + 1)
                    to = sdst_bank[0:BP, k * BP:(k + 1) * BP] if k < 4 else sdst_last[0:BP, :]
                    last = nc.tensor.matmul(to, ones_f[0:BP, 0:BP], diag[:, k, :], start=True, stop=True)
                last.then_inc(sdst_done, 1)

            for i in range(7):
                project(i)
            pe.wait_ge(small_loaded, 48)
            nc.tensor.transpose(b1_ps, b1_row[:, :], ident[0:NE * KB, 0:NE * KB])
            pe.wait_ge(bad_made, 1)
            nc.tensor.matmul(bad_sum, bad[:, :], ones_f[:, 0:1], start=True, stop=True, skip_group_check=True)
            for k in range(KB):
                last = nc.tensor.matmul(wr_ps, ones_f[:, 0:BP], wr_sb[:, k, :], start=(k == 0), stop=(k == KB - 1),
                                        skip_group_check=True)
            last.then_inc(small_summed, 1)
            repeat_sdst()
            project(7)

            def opens_bank(g):
                if g < 2:
                    pe.wait_ge(bad_flag, 1)
                    pe.wait_ge(b1T_ready, 1)
                    pe.wait_ge(minus_wr_ready, 1)
                    pe.wait_ge(keys_copied, 1)
                elif 2 < g < NG - 1:
                    pe.wait_ge(h_copied, len(HALVES))
                elif g == NG - 1:
                    pe.wait_ge(wt_done, 1)

            opened = set()

            def count(c):
                s, q = c % RING, c // BAT
                if c % BAT == 0:
                    pe.wait_ge(onehots_made, q + 1)
                lo = (c * STEP - BEFORE) * NB
                hi = lo + WC
                g0, g1 = max(lo, 0) // GW, min(hi - 1, N * NB - 1) // GW
                for g in range(g0, g1 + 1):
                    c0, c1 = max(lo, g * GW, 0), min(hi, (g + 1) * GW, N * NB)
                    if g not in opened:
                        opens_bank(g)
                    ins = nc.tensor.matmul(count_bank[g][:, c0 - g * GW:c1 - g * GW], ring[:, s, 0:CH],
                                           ring[:, s, CH + c0 - lo:CH + c1 - lo], start=g not in opened, stop=False,
                                           skip_group_check=True)
                    opened.add(g)
                    if g == g0 and (c == NCH - 1 or (lo + STEP * NB) // GW > g0 >= 0 and lo >= 0):
                        ins.then_inc(counts_done, 1)
                        if g1 == g0 and c % BAT == BAT - 1:
                            pe.sem_inc(onehots_free, 1)
                    elif g == g1 and c % BAT == BAT - 1:
                        ins.then_inc(onehots_free, 1)

            def aggregate(b, k):
                if k == 0:
                    pe.wait_ge(wt_done, min(-(-BP * (b + 1) // GN), NG))
                    if b == 0:
                        pe.wait_ge(consts_made, ONES_COLUMN)
                        pe.wait_ge(sd_low_ready, 1)
                    if b >= 2:
                        pe.wait_ge(x2_ready, b - 1)
                if b == 0:
                    pe.wait_ge(h_biased, NB + k + 1)
                last = multiply(b, k)
                if k == NB - 1:
                    last.then_inc(agg_done, 1)

            def multiply(b, k):
                pa, pc = agg_bank[b % 2]
                lhs = wt[:, k, b * BP:(b + 1) * BP]
                nc.tensor.matmul(pa[0:BP, 0:HH], lhs, hx[:, k, 0:HH], start=(k == 0), stop=(k == NB - 1))
                return nc.tensor.matmul(pc[0:BP, 0:HH + 1], lhs, hx[:, k, HH:2 * HH + 1], start=(k == 0), stop=(k == NB - 1))

            for c in range(NCH):
                count(c)
                if c in LATE_H:
                    project(8 + LATE_H.index(c))
                for i, at in enumerate(EARLY_AGG):
                    if at == c:
                        aggregate(i // NB, i % NB)

            pe.wait_ge(bad_flag, 1)
            outside = pe.value_load(flags[0:1, 0:1])
            with pe.If(outside != 0):
                pe.wait_ge(wt_done, NG)
                with pe.Fori(0, NG) as g:
                    pe.wait_ge(gen_wt, g * 2 + 1)
                    nc.tensor.matmul(gen_bank[:, :], zeros_b[:, 0:128], zeros_b[:, :], start=True, stop=False,
                                     skip_group_check=True)
                    with pe.Fori(0, NCH) as c:
                        pe.wait_ge(gen_made, g * NCH + c + 1)
                        nc.tensor.matmul(gen_bank[:, 0:GW], gen_a[:, :], gen_b[:, :], start=False, stop=False,
                                         skip_group_check=True).then_inc(gen_used, 1)
                    nc.tensor.matmul(gen_bank[:, :], zeros_b[:, 0:128], zeros_b[:, :], start=False, stop=True,
                                     skip_group_check=True).then_inc(gen_counted, 1)
                pe.wait_ge(gen_wt, NG * 2 + 1)
                for k in range(NB):
                    multiply(0, k).then_inc(first_redone, 1)

            def turn2(b):
                pe.wait_ge(x2_ready, b + 1)
                if b == 0:
                    pe.wait_ge(wt_done, NG)
                if b >= 1:
                    pe.wait_ge(xn2T_ready, b)
                for k in range(KB):
                    last = nc.tensor.transpose(turn2_bank[:, k * BP:(k + 1) * BP], rows[:, b, k * 128:(k + 1) * 128],
                                               ident[0:BP, 0:BP])
                last.then_inc(xn2_turned, 1)

            def route(b):
                pe.wait_ge(xn2T_ready, b + 1)
                if b >= 1:
                    pe.wait_ge(hot_ready, b)
                for k in range(KB):
                    last = nc.tensor.matmul(logit_bank[0:BP, b * NE:(b + 1) * NE], xnT[:, k, b * BP:(b + 1) * BP],
                                            wr_sb[:, k, :], start=(k == 0), stop=(k == KB - 1))
                last.then_inc(logits_done, 1)

            def order(b):
                pe.wait_ge(hot_ready, b + 1)
                if b >= 1:
                    pe.wait_ge(slots_ready, b)
                to = rank_bank[0:BP, b * NE:(b + 1) * NE]
                for t in range(b):
                    nc.tensor.matmul(to, ones_b[0:BP, 0:BP], hot[:, t, :], start=(t == 0), stop=False)
                nc.tensor.matmul(to, lower[:, :], hot[:, b, :], start=(b == 0), stop=True).then_inc(ranks_done, 1)

            pe.wait_ge(consts_made, ORDER)
            for b in range(NB):
                for k in range(NB):
                    if b * NB + k < len(EARLY_AGG):
                        continue
                    if b >= 1 and k == 2:
                        turn2(b - 1)
                    if b >= 1 and k == 3:
                        route(b - 1)
                    if b >= 2 and k == 1:
                        order(b - 2)
                    aggregate(b, k)
            def place(b):
                pe.wait_ge(placed, b + 1)
                pe.wait_ge(xn2_ready, b + 1)
                for k in range(KB):
                    last = nc.tensor.matmul(xsT_bank[0][:, k * CAP:(k + 1) * CAP], xn[:, b, k * 128:(k + 1) * 128],
                                            place0[:, b, :], start=(b == 0 and k == 0), stop=(b == NB - 1),
                                            skip_group_check=True)
                if b == NB - 1:
                    last.then_inc(xs_turned, 1)

            order(NB - 2)
            place(0)
            place(1)
            turn2(NB - 1)
            place(2)
            route(NB - 1)
            place(3)
            keep_busy(BUSY_GAP, pb[5])
            order(NB - 1)
            place(NB - 1)
            pe.wait_ge(over_made, 1)
            nc.tensor.matmul(over_sum, novr[:, :], ones_f[0:BP, 0:1], start=True, stop=True).then_inc(over_summed, 1)

            def round_pe(r):
                static = isinstance(r, int)

                def n(e):
                    return r * NE + e + 1

                def turn(e):
                    pe.wait_ge(xs_n_ready, n(e))
                    if not (static and e < 2):
                        pe.wait_ge(xsT_ready, n(e) - 2)
                    for k in range(KB):
                        last = nc.tensor.transpose(xsT_bank[e % 2][:, k * CAP:(k + 1) * CAP],
                                                   xs_n[:, e % 2, k * 128:(k + 1) * 128], ident[:, :])
                    last.then_inc(xs_turned, 1)

                def layer1(e):
                    pe.wait_ge(xsT_ready, n(e))
                    pe.wait_ge(w_loaded[e], r * 32 + 32)
                    if not (static and e < 2):
                        pe.wait_ge(relu_act, n(e) - 2)
                        pe.wait_ge(relu_dve, n(e) - 2)
                    for f in range(KB):
                        to = l1_bank[e % 2][f // 2][:, (f % 2) * CAP:(f % 2 + 1) * CAP]
                        for k in range(KB):
                            last = nc.tensor.matmul(to,
                                                    w1_sb[:, e % WBUF, k, f * 128:(f + 1) * 128], xsT[:, e % 2, k, :],
                                                    start=(k == 0), stop=(k == KB - 1))
                        if f == 1:
                            last.then_inc(l1_half, 1)
                    last.then_inc(l1_done, 1)

                def layer2(e, between=None):
                    pe.wait_ge(relu_act, n(e))
                    pe.wait_ge(relu_dve, n(e))
                    if not (static and e < 2):
                        pe.wait_ge(y_ready, n(e) - 2)
                    to = l2_bank[e % 2][:, :]
                    if static and e in SPLIT:
                        pe.wait_ge(h1_split, e - SPLIT_FROM + 1)
                        pe.wait_ge(w2_split, e - SPLIT_FROM + 1)
                    for f in range(KB):
                        if f == KB // 2 and between:
                            between()
                        if static and e in SPLIT:
                            hi, w_hi = h1_hi[:, e % 2, f, :], w2_hi[e % 2][:, f, :]
                            nc.tensor.matmul(to, hi, w_hi, start=(f == 0), stop=False)
                            nc.tensor.matmul(to, hi, w2_lo[:, e % WBUF, f, :], start=False, stop=False)
                            last = nc.tensor.matmul(to, h1_lo[:, e % 2, f, :], w_hi, start=False, stop=(f == KB - 1))
                        else:
                            last = nc.tensor.matmul(to, h1T[:, e % 2, f, :], w2_sb[:, e % WBUF, f, :],
                                                    start=(f == 0), stop=(f == KB - 1))
                    last.then_inc(l2_done, 1)

                if static:
                    layer1(0)
                    layer2(0, between=lambda: turn(1))
                    turn(2)
                else:
                    turn(0)
                for e in range(1 if static else 0, NE):
                    layer1(e)
                    if e + 1 < NE and not (static and e == 1):
                        turn(e + 1)
                    if e >= (2 if static else 1):
                        layer2(e - 1)
                layer2(NE - 1)

            keep_busy(BUSY_GAP, pb[5])
            pe.wait_ge(over_flag, 1)
            round_pe(0)
            more = pe.value_load(flags[0:1, 1:2])
            with pe.If(more != 0):
                with pe.Fori(1, ROUNDS) as r:
                    round_pe(r)


_INS = ['x', 'src', 'dst', 'L0_gnn_W', 'L0_gnn_b_w', 'L0_gnn_a', 'L0_gnn_b_a', 'L0_ffn_Wr', 'L0_ffn_br', 'L0_ffn_W1',
        'L0_ffn_b1', 'L0_ffn_W2', 'L0_ffn_b2']


def kernel(**inputs):
    import numpy as _np
    import concourse.bacc as _bacc
    from concourse import mybir as _mybir
    from concourse.bass_utils import run_bass_kernel_spmd as _run

    nc = _bacc.Bacc("TRN2", target_bir_lowering=False, num_devices=1)
    arrays, args = {}, []
    for name in _INS:
        a = _np.ascontiguousarray(inputs[name])
        if a.ndim == 0:
            a = a.reshape(1)
        arrays[f"in_{name}_dram"] = a
        args.append(nc.dram_tensor(f"in_{name}_dram", a.shape, _mybir.dt.from_np(a.dtype), kind="ExternalInput").ap())
    args.append(nc.dram_tensor("out_0_dram", (N, D), _mybir.dt.float32, kind="ExternalOutput").ap())
    gnn_ffn(nc, *args)
    r = _run(nc, [arrays], core_ids=[0])
    return r.results[0]["out_0_dram"]
```
